# Optimizing a Trainium2 kernel written in Bass

```python
import numpy as np
import jax
import jax.numpy as jnp

def _softmax(x, axis=-1):
    return jax.nn.softmax(x, axis=axis)

def _gelu(x):
    return jax.nn.gelu(x, approximate=True)

def _silu(x):
    return jax.nn.silu(x)

def _sigmoid(x):
    return jax.nn.sigmoid(x)

def _layernorm(x, axis=-1, eps=1e-05):
    m = jnp.mean(x, axis=axis, keepdims=True)
    v = jnp.var(x, axis=axis, keepdims=True)
    return (x - m) / jnp.sqrt(v + eps)

def _scatter_add(tgt, idx, src, axis=0):
    return tgt.at[idx].add(src)

def _segment_sum(src, seg, n):
    return jax.ops.segment_sum(src, seg, n)
kernel_name = 'mk_xattn_ffn_d1_seqx_r4_b990bf'

def setup_inputs(seed: int=0):
    np.random.seed(seed)
    _w = jnp.asarray

    def _rec_inputs():
        import jax
        import jax.numpy as jnp
        _rk = jax.random.key(seed)
        x = -0.000125 + 0.9999 * jax.random.normal(jax.random.fold_in(_rk, 1), (4, 512, 512), jnp.float32)
        _lenS = 512 - jax.random.randint(jax.random.fold_in(_rk, 7), (4,), 0, max(1, 512 // 4) + 1, jnp.int32)
        _lenS2 = 1024 - jax.random.randint(jax.random.fold_in(_rk, 8), (4,), 0, max(1, 1024 // 4) + 1, jnp.int32)
        _ctx_2048P = jax.random.normal(jax.random.fold_in(_rk, 11), (4, 16, 512), jnp.float32)
        _ctx_2048c = jax.random.dirichlet(jax.random.fold_in(_rk, 511), 0.3 * jnp.ones((16,), jnp.float32), (4, 1024))
        _ctx_2048t = jnp.einsum('bsk,bkd->bsd', _ctx_2048c, _ctx_2048P)
        _ctx_2048t = _ctx_2048t * jax.lax.rsqrt(jnp.mean(jnp.square(_ctx_2048t)) + 1e-12) * 0.953939
        ctx_2048 = -1.52775e-05 + 0.999936 * (_ctx_2048t + 0.3 * jax.random.normal(jax.random.fold_in(_rk, 611), (4, 1024, 512), jnp.float32))
        return (x, ctx_2048)
    x, ctx_2048 = _rec_inputs()

    def _L0_xattn_setup():
        import jax, jax.numpy as jnp
        import numpy as np
        EPS = 1e-06
        NUM_HEADS = 16

        def _feature_map(x):
            return jnp.where(x > 0, x + 1.0, jnp.exp(x))
        key = jax.random.key(seed)
        ks = jax.random.split(key, 7)
        B, L, S, D = (4, 1024, 1024, 512)
        sc = 1.0 / np.sqrt(D)
        return {'query': jax.random.normal(ks[0], (B, L, D), jnp.float32), 'kv': jax.random.normal(ks[1], (B, S, D), jnp.float32), 'Wq': jax.random.normal(ks[2], (D, D), jnp.float32) * sc, 'Wg': jax.random.normal(ks[3], (D, D), jnp.float32) * sc, 'bg': jnp.ones((D,), jnp.float32), 'Wkv': jax.random.normal(ks[4], (2 * D, D), jnp.float32) * sc, 'Wo': jax.random.normal(ks[5], (D, D), jnp.float32) * sc}
    _L0_xattn_all = _L0_xattn_setup()
    _L0_xattn_in = {k: v for k, v in _L0_xattn_all.items() if k in ('Wq', 'Wg', 'bg', 'Wkv', 'Wo')}
    del _L0_xattn_all

    def _L0_ffn_setup():
        import jax, jax.numpy as jnp
        import numpy as np
        K_TOP = 2
        key = jax.random.key(seed)
        k0, k1, k2 = jax.random.split(key, 3)
        B, S, D, E, F = (4, 512, 512, 8, 512)
        x = jax.random.normal(k0, (B, S, D), dtype=jnp.float32)
        Wr = jax.random.normal(k1, (D, E), dtype=jnp.float32) * 0.02
        We = jax.random.normal(k2, (E, D, F), dtype=jnp.float32) * 0.02
        be = jnp.zeros((E, F), dtype=jnp.float32)
        return {'x': x, 'Wr': Wr, 'We': We, 'be': be}
    _L0_ffn_all = _L0_ffn_setup()
    _L0_ffn_in = {k: v for k, v in _L0_ffn_all.items() if k in ('Wr', 'We', 'be')}
    del _L0_ffn_all
    return {'x': x, 'ctx_2048': ctx_2048, 'L0_xattn_Wq': _L0_xattn_in['Wq'], 'L0_xattn_Wg': _L0_xattn_in['Wg'], 'L0_xattn_bg': _L0_xattn_in['bg'], 'L0_xattn_Wkv': _L0_xattn_in['Wkv'], 'L0_xattn_Wo': _L0_xattn_in['Wo'], 'L0_ffn_Wr': _L0_ffn_in['Wr'], 'L0_ffn_We': _L0_ffn_in['We'], 'L0_ffn_be': _L0_ffn_in['be']}

def reference(x, ctx_2048, L0_xattn_Wq, L0_xattn_Wg, L0_xattn_bg, L0_xattn_Wkv, L0_xattn_Wo, L0_ffn_Wr, L0_ffn_We, L0_ffn_be):
    import jax
    import jax.numpy as jnp

    def _L0_xattn_ref(query, kv, Wq, Wg, bg, Wkv, Wo):
        import jax, jax.numpy as jnp
        import numpy as np
        EPS = 1e-06
        NUM_HEADS = 16

        def _feature_map(x):
            return jnp.where(x > 0, x + 1.0, jnp.exp(x))
        B, L, D = query.shape
        S = kv.shape[1]
        H = NUM_HEADS
        hd = D // H
        q = query @ Wq.T
        gate = jax.nn.sigmoid(query @ Wg.T + bg)
        kvp = kv @ Wkv.T
        k, v = jnp.split(kvp, 2, axis=-1)
        q = _feature_map(q.reshape(B, L, H, hd).transpose(0, 2, 1, 3))
        k = _feature_map(k.reshape(B, S, H, hd).transpose(0, 2, 1, 3))
        v = v.reshape(B, S, H, hd).transpose(0, 2, 1, 3)
        kv_summary = jnp.einsum('bhsd,bhse->bhde', k, v)
        k_sum = k.sum(axis=-2)
        z = 1.0 / (jnp.einsum('bhld,bhd->bhl', q, k_sum)[..., None] + EPS)
        attn = jnp.einsum('bhld,bhde->bhle', q, kv_summary) * z
        attn = attn.transpose(0, 2, 1, 3).reshape(B, L, D)
        out = attn * gate @ Wo.T
        return out

    def _L0_ffn_ref(x, Wr, We, be):
        import jax, jax.numpy as jnp
        import numpy as np
        K_TOP = 2
        logits = jnp.einsum('bsd,de->bse', x, Wr)
        w, sel = jax.lax.top_k(logits, K_TOP)
        w = jax.nn.softmax(w, axis=-1)
        E = We.shape[0]
        gate = jnp.einsum('bsk,bske->bse', w, jax.nn.one_hot(sel, E, dtype=w.dtype))
        out = jnp.zeros(x.shape[:2] + (We.shape[2],), dtype=x.dtype)
        for e in range(E):
            out = out + gate[..., e:e + 1] * (jnp.einsum('bsd,df->bsf', x, We[e]) + be[e])
        return out
    x = x + _L0_xattn_ref(_layernorm(x, axis=-1), ctx_2048, L0_xattn_Wq, L0_xattn_Wg, L0_xattn_bg, L0_xattn_Wkv, L0_xattn_Wo)
    x = x + _L0_ffn_ref(_layernorm(x, axis=-1), L0_ffn_Wr, L0_ffn_We, L0_ffn_be)
    return x

_drawn_inputs = setup_inputs


def setup_inputs(seed=0):
    import zlib

    import numpy as np

    out = dict(_drawn_inputs(seed))
    spreads = {'L0_xattn_bg': (1.0, 0.2), 'L0_ffn_be': (0.0, 0.1)}
    factors = {}
    for name, (base, spread) in spreads.items():
        noise = np.random.default_rng([zlib.crc32(name.encode()), seed]).standard_normal(out[name].shape)
        drawn = base * np.exp(spread * noise) if base else spread * noise
        out[name] = jnp.asarray(drawn.astype(out[name].dtype))
    for name, factor in factors.items():
        out[name] = (out[name] * factor).astype(out[name].dtype)
    return out
```

```python
from contextlib import ExitStack

import concourse.bass as bass
from concourse import mybir

F32 = mybir.dt.float32
F32R = mybir.dt.float32r
U32 = mybir.dt.uint32
ALU = mybir.AluOpType
ACT = mybir.ActivationFunctionType

P = 128
HEADS = 16
ATTN_EPS = 1e-6
NORM_EPS = 1e-5


def xattn_moe_kernel(nc, x, ctx_in, wq, wg, bg, wkv, wo, wr, we, be, out):
    B, L, D = x.shape
    S = ctx_in.shape[1]
    E = we.shape[0]
    KT = D // P
    ST = S // P
    TT = L // P
    G = D // P
    HG = HEADS // G
    HD = D // HEADS
    CW = P + HG
    assert L == D == 512 and S % (2 * P) == 0 and E == 8

    with ExitStack() as stack:
        def sb(name, shape, dt=F32):
            return stack.enter_context(nc.sbuf_tensor(name, shape, dt))

        def sem(name):
            return stack.enter_context(nc.semaphore(name))

        wraw = sb("wraw", [P, 2, 4, D])
        w_hi = sb("w_hi", [P, 5, KT, D], F32R)
        w_lo = sb("w_lo", [P, 5, KT, D], F32R)
        WK, WV, WQ, WG, WO = range(5)
        wr_sb = sb("wr_sb", [P, KT, E])
        bias_raw = sb("bias_raw", [64, D])
        bias = sb("bias", [64, D], F32R)
        pick = sb("pick", [64, 1 + E, P], F32R)
        ident = sb("ident", [P, P])
        mask = sb("mask", [P, CW])
        iota8 = sb("iota8", [P, E])
        mhalf = sb("mhalf", [P, TT])
        ctx_raw = sb("ctx_raw", [P, 2, 2, D])
        ctxT_hi = sb("ctxT_hi", [P, 2, KT, P], F32R)
        ctxT_lo = sb("ctxT_lo", [P, 2, KT, P], F32R)
        expk = sb("expk", [P, 2, D])
        khat = sb("khat", [P, 2, D])
        vones = sb("vones", [P, 2, G, CW])
        kvbd = sb("kvbd", [P, G, CW])
        x_raw = sb("x_raw", [P, TT, D])
        xn = sb("xn", [P, 2, D])
        xT_hi = sb("xT_hi", [P, KT, L], F32R)
        xT_lo = sb("xT_lo", [P, KT, L], F32R)
        expq = expk
        qhat = sb("qhat", [P, G, L])
        gate = sb("gate", [P, TT, D])
        pick_raw = gate[0:64, :, :].rearrange("p t d -> p (t d)")[:, 0:(1 + E) * P].rearrange("p (n c) -> p n c", n=1 + E)
        num = sb("num", [P, 2, D])
        ag = sb("ag", [P, 2, D])
        agT_hi = sb("agT_hi", [P, 2, KT, P], F32R)
        agT_lo = sb("agT_lo", [P, 2, KT, P], F32R)
        x2 = sb("x2", [P, TT, D])
        x2n = xn
        x2T = qhat[:, :, :].rearrange("p t (k c) -> p t k c", k=KT)
        stats = sb("stats", [P, 6])
        mv = sb("mv", [P, 2, TT, 2])
        rstd = sb("rstd", [P, 2, TT])
        den = sb("den", [P, 2, HEADS])
        z = sb("z", [P, 2, HEADS])
        route = sb("route", [P, 64])
        routei = sb("routei", [P, 8], U32)
        egate = sb("egate", [P, TT, E])

        tp = [stack.enter_context(nc.psum_tensor(f"tp{i}", [P, KT, P], F32)) for i in range(2)]
        pj = [stack.enter_context(nc.psum_tensor(f"pj{i}", [P, D], F32)) for i in range(4)]
        kvp = [stack.enter_context(nc.psum_tensor(f"kvp{i}", [P, 2, CW], F32)) for i in range(2)]

        w_loaded = [sem(f"w_loaded{i}") for i in range(2)]
        small_loaded = sem("small_loaded")
        x_loaded = sem("x_loaded")
        ctx_loaded = [sem(f"ctx_loaded{i}") for i in range(2)]
        we_loaded = [sem(f"we_loaded{i}") for i in range(2)]
        stored = sem("stored")
        consts = sem("consts")
        turned, hi_done, lo_done = sem("turned"), sem("hi_done"), sem("lo_done")
        k_done, v_done, kv_done = sem("k_done"), sem("v_done"), sem("kv_done")
        q_done, g_done, at_done = sem("q_done"), sem("g_done"), sem("at_done")
        wo_done, logit_done, moe_done = sem("wo_done"), sem("logit_done"), sem("moe_done")
        expk_done, mink_done, khat_done, v_copied = sem("expk_done"), sem("mink_done"), sem("khat_done"), sem("v_copied")
        kvbd_done = sem("kvbd_done")
        expq_done, minq_done, qhat_done, gate_done = sem("expq_done"), sem("minq_done"), sem("qhat_done"), sem("gate_done")
        mean_done, xn_done = sem("mean_done"), sem("xn_done")
        num_done, ag_done = sem("num_done"), sem("ag_done")
        x2_done, mean2_done, x2n_done = sem("x2_done"), sem("mean2_done"), sem("x2n_done")
        logit_copied, gap_done, gap_exp = sem("logit_copied"), sem("gap_done"), sem("gap_exp")
        egate_done = sem("egate_done")
        acc_done = sem("acc_done")
        dve_passed, pool_passed = sem("dve_passed"), sem("pool_passed")
        dve_step, pool_step = sem("dve_step"), sem("pool_step")

        UNITS = ST + 3 * TT
        PER = {
            "turned": UNITS, "hi": UNITS, "lo": UNITS, "k": ST, "v": ST, "kv": 1, "q": G, "g": TT,
            "at": TT, "wo": TT, "logit": TT, "moe": E * TT, "expk": ST, "mink": ST, "khat": ST,
            "v_copied": ST, "kvbd": 1, "expq": G, "minq": G, "qhat": G, "gate": TT, "mean": 1, "xn": TT,
            "num": TT, "ag": TT, "x2": TT, "mean2": TT, "x2n": TT, "logit_copied": TT, "gap": TT,
            "gap_exp": TT, "egate": TT, "acc": E * TT,
        }
        SEMS = {
            "turned": turned, "hi": hi_done, "lo": lo_done, "k": k_done, "v": v_done, "kv": kv_done,
            "q": q_done, "g": g_done, "at": at_done, "wo": wo_done, "logit": logit_done, "moe": moe_done,
            "expk": expk_done, "mink": mink_done, "khat": khat_done, "v_copied": v_copied,
            "kvbd": kvbd_done, "expq": expq_done, "minq": minq_done, "qhat": qhat_done,
            "gate": gate_done, "mean": mean_done, "xn": xn_done, "num": num_done, "ag": ag_done,
            "x2": x2_done, "mean2": mean2_done, "x2n": x2n_done, "logit_copied": logit_copied,
            "gap": gap_done, "gap_exp": gap_exp, "egate": egate_done, "acc": acc_done,
        }

        def nth(name, b, i):
            return (b + 1) * PER[name] + i + 1

        USES = []
        for i in range(ST):
            USES += [("khat", i), ("v_copied", i)]
        USES += [("qhat", g) for g in range(G)]
        USES += [("gate", t) for t in range(TT)]
        for t in range(TT):
            USES += [("num", t), ("num", t)]
        USES += [("x2", t) for t in range(TT)]
        USES += [("logit_copied", t) for t in range(TT)]
        USES += [("acc", i) for i in range(E * TT)]
        assert len(USES) % 4 == 0
        FIRST_Q, FIRST_G = 2 * ST, 2 * ST + G
        FIRST_AT = FIRST_G + TT
        FIRST_WO = FIRST_AT + 2 * TT
        FIRST_LOGIT = FIRST_WO + TT
        FIRST_MOE = FIRST_LOGIT + TT
        X0, AG0, Z0 = ST, ST + TT, ST + 2 * TT

        block = stack.enter_context(nc.Block())

        @block.sync
        def _(sp):
            srcs = [wkv[0:D, :], wkv[D:2 * D, :], wq, wg, wo]
            for n, src in enumerate(srcs):
                if n >= 2:
                    sp.wait_ge(lo_done, KT * (n - 1))
                sp.dma_start(wraw[:, n % 2, :, :], src.rearrange("(a p) d -> p a d", p=P)).then_inc(w_loaded[n % 2], 16)
                if n == 0:
                    sp.dma_start(wr_sb[:, :, :], wr.rearrange("(k p) e -> p k e", p=P)).then_inc(small_loaded, 16)
                    sp.wait_ge(consts, 1)
                    for row in (0, 32):
                        sp.dma_start(bias_raw[row:row + 1, :], bg.rearrange("(a d) -> a d", a=1)).then_inc(small_loaded, 16)
                        sp.dma_start(bias_raw[row + 1:row + 1 + E, :], be).then_inc(small_loaded, 16)
            sp.wait_ge(lo_done, 5 * KT)
            with sp.Fori(0, B) as b:
                sp.wait_ge(x2_done, nth("x2", b, -1))
                sp.dma_start(x_raw[:, :, :], x[b, :, :].rearrange("(t p) d -> p t d", p=P)).then_inc(x_loaded, 16)
                for j in range(ST // 2):
                    sp.wait_ge(lo_done, nth("lo", b, 2 * j - 3) if j >= 2 else nth("lo", b, -1))
                    sp.dma_start(ctx_raw[:, j % 2, :, :],
                                 ctx_in[b, 2 * j * P:(2 * j + 2) * P, :].rearrange("(t p) d -> p t d", p=P)).then_inc(ctx_loaded[j % 2], 16)
                for e in range(E):
                    sp.wait_ge(moe_done, nth("moe", b, (e - 1) * TT - 1))
                    sp.dma_start(wraw[:, e % 2, :, :], we[e, :, :].rearrange("(k p) f -> p k f", p=P)).then_inc(we_loaded[e % 2], 16)
                for t in range(TT):
                    sp.wait_ge(acc_done, nth("acc", b, (E - 1) * TT + t))
                    sp.dma_start(out[b, t * P:(t + 1) * P, :], x2[:, t, :]).then_inc(stored, 16)
            sp.wait_ge(stored, 16 * B * TT)

        @block.gpsimd
        def _(pool):
            for name in ("mink", "minq", "xn", "x2n", "ag"):
                pool.sem_inc(SEMS[name], PER[name])
            nc.gpsimd.memset(bias_raw[:, :], 0.0).then_inc(consts, 1)
            nc.gpsimd.memset(ident[:, :], 0.0).then_inc(pool_step, 1)
            nc.gpsimd.memset(mask[:, :], 1.0).then_inc(pool_step, 1)
            nc.gpsimd.memset(pick_raw[:, :, :], 0.0).then_inc(pool_step, 1)
            nc.gpsimd.memset(mhalf[:, :], -0.5).then_inc(pool_step, 1)
            nc.gpsimd.memset(vones[:, :, :, P:CW], 1.0).then_inc(consts, 1)
            nc.gpsimd.iota(iota8[:, :], pattern=[[1, E]], base=0, channel_multiplier=0,
                           allow_small_or_imprecise_dtypes=True).then_inc(consts, 1)
            pool.wait_ge(pool_step, 4)
            for row in (0, 32):
                nc.gpsimd.affine_select(out=pick_raw[:, :, :], in_=pick_raw[:, :, :], compare_op=ALU.not_equal, fill=1.0,
                                        base=-row, pattern=[[-1, 1 + E], [0, P]], channel_multiplier=1).then_inc(pool_step, 1)
                pool.wait_ge(pool_step, 5 + row // 32)
            nc.gpsimd.tensor_copy(pick[:, :, :], pick_raw[:, :, :]).then_inc(consts, 1)
            nc.gpsimd.affine_select(out=ident[:, :], in_=ident[:, :], compare_op=ALU.not_equal, fill=1.0,
                                    base=0, pattern=[[-1, P]], channel_multiplier=1).then_inc(consts, 1)
            m4 = mask[:, 0:P].rearrange("p (h e) -> p h e", h=HG)
            for n, (ap, pat) in enumerate(((m4, [[-HD, HG], [0, HD]]), (mask[:, P:CW], [[-HD, HG]]))):
                nc.gpsimd.affine_select(out=ap, in_=ap, compare_op=ALU.is_ge, fill=0.0, base=0,
                                        pattern=pat, channel_multiplier=1).then_inc(pool_step, 1)
                pool.wait_ge(pool_step, 7 + 2 * n)
                nc.gpsimd.affine_select(out=ap, in_=ap, compare_op=ALU.is_ge, fill=0.0, base=HD - 1,
                                        pattern=[[-s, c] for s, c in pat], channel_multiplier=-1).then_inc(pool_step, 1)
                pool.wait_ge(pool_step, 8 + 2 * n)
            nc.gpsimd.memset(rstd[:, :, :], 0.0).then_inc(consts, 1)

            STEPS = 2 + 2 * TT
            base = 10

            with pool.Fori(0, B) as b:
                def rsqrt(slot, t0, nt, k):
                    pool.sem_inc(pool_passed, 1)
                    nc.gpsimd.tensor_scalar(rstd[:, slot, t0:t0 + nt], mv[:, slot, t0:t0 + nt, 1], NORM_EPS, None,
                                            ALU.add).then_inc(pool_step, 1)
                    pool.wait_ge(pool_step, b * STEPS + base + k + 1)
                    nc.gpsimd.tensor_tensor(rstd[:, slot, t0:t0 + nt], rstd[:, slot, t0:t0 + nt], mhalf[:, 0:nt],
                                            ALU.pow).then_inc(pool_step, 1)
                    pool.wait_ge(pool_step, b * STEPS + base + k + 2)

                def after_wait():
                    pool.sem_inc(pool_passed, 1)

                def min_k(i):
                    pool.wait_ge(expk_done, nth("expk", b, i))
                    after_wait()
                    nc.gpsimd.tensor_scalar(expk[:, i % 2, :], expk[:, i % 2, :], 1.0, None, ALU.min).then_inc(mink_done, 1)

                def norm_x(t):
                    pool.wait_ge(turned, nth("turned", b, X0 + t - 2 if t >= 2 else -1))
                    after_wait()
                    nc.gpsimd.tensor_scalar(xn[:, t % 2, :], x_raw[:, t, :], mv[:, 0, t, 0:1], rstd[:, 0, t:t + 1],
                                            ALU.subtract, ALU.mult).then_inc(xn_done, 1)

                for i in range(ST):
                    min_k(i)
                    if i == 3:
                        pool.wait_ge(mean_done, nth("mean", b, 0))
                        rsqrt(0, 0, TT, 0)
                    if i == ST - 4:
                        norm_x(0)
                    if i == ST - 3:
                        norm_x(1)
                        norm_x(2)
                    if i == ST - 2:
                        norm_x(3)
                for g in range(G):
                    pool.wait_ge(expq_done, nth("expq", b, g))
                    after_wait()
                    nc.gpsimd.tensor_scalar(expq[:, g % 2, :], expq[:, g % 2, :], 1.0, None, ALU.min).then_inc(minq_done, 1)
                for t in range(TT):
                    pool.wait_ge(num_done, nth("num", b, t))
                    pool.wait_ge(gate_done, nth("gate", b, t))
                    pool.wait_ge(turned, nth("turned", b, AG0 + t - 2 if t >= 2 else -1))
                    nc.gpsimd.tensor_tensor(ag[:, t % 2, :], num[:, t % 2, :], gate[:, t, :], ALU.mult).then_inc(ag_done, 1)
                for t in range(TT):
                    pool.wait_ge(mean2_done, nth("mean2", b, t))
                    rsqrt(1, t, 1, 2 + 2 * t)
                    pool.wait_ge(turned, nth("turned", b, Z0 + t - 2 if t >= 2 else -1))
                    after_wait()
                    nc.gpsimd.tensor_scalar(x2n[:, t % 2, :], x2[:, t, :], mv[:, 1, t, 0:1], rstd[:, 1, t:t + 1],
                                            ALU.subtract, ALU.mult).then_inc(x2n_done, 1)

        @block.scalar
        def _(act):
            for name in ("hi", "expk", "v_copied", "expq", "gate", "gap_exp"):
                if name != "hi":
                    act.sem_inc(SEMS[name], PER[name])
            for n in range(5):
                for k in range(KT):
                    act.wait_ge(turned, n * KT + k + 1)
                    nc.scalar.copy(w_hi[:, n, k, :], tp[(n * KT + k) % 2][:, :, :].rearrange("p a c -> p (a c)")).then_inc(hi_done, 1)

            with act.Fori(0, B) as b:
                def high(u, dst):
                    act.wait_ge(turned, nth("turned", b, u))
                    nc.scalar.copy(dst, tp[u % 2][:, :, :]).then_inc(hi_done, 1)

                def high_c(i):
                    act.wait_ge(v_done, nth("v", b, i - 2))
                    high(i, ctxT_hi[:, i % 2, :, :])

                def high_x(t):
                    high(X0 + t, xT_hi[:, :, t * P:(t + 1) * P])

                for i in range(ST):
                    if i == 0:
                        high_c(0)
                    if i + 1 < ST:
                        high_c(i + 1)
                    if i == ST - 2:
                        high_x(0)
                    if i == ST - 1:
                        high_x(1)
                        high_x(2)
                    act.wait_ge(k_done, nth("k", b, i))
                    act.wait_ge(khat_done, nth("khat", b, i - 2)) if i >= 2 else act.wait_ge(qhat_done, nth("qhat", b, i - 2))
                    nc.scalar.activation(expk[:, i % 2, :], pj[(2 * i) % 4][:, :], ACT.Exp).then_inc(expk_done, 1)
                    act.wait_ge(v_done, nth("v", b, i))
                    if i >= 2:
                        act.wait_ge(kv_done, b * ST + i - 1)
                    nc.scalar.copy(vones[:, i % 2, :, 0:P], pj[(2 * i + 1) % 4][:, :].rearrange("p (g c) -> p g c", g=G)).then_inc(v_copied, 1)
                high_x(3)
                for g in range(G):
                    act.wait_ge(q_done, nth("q", b, g))
                    act.wait_ge(qhat_done, nth("qhat", b, g - 2)) if g >= 2 else act.wait_ge(khat_done, nth("khat", b, ST + g - 2))
                    nc.scalar.activation(expq[:, g % 2, :], pj[(FIRST_Q + g) % 4][:, :], ACT.Exp).then_inc(expq_done, 1)
                for t in range(TT):
                    act.wait_ge(g_done, nth("g", b, t))
                    nc.scalar.activation(gate[:, t, :], pj[(FIRST_G + t) % 4][:, :], ACT.Sigmoid).then_inc(gate_done, 1)
                for t in range(TT):
                    act.wait_ge(wo_done, nth("wo", b, t - 2))
                    high(AG0 + t, agT_hi[:, t % 2, :, :])
                for t in range(TT):
                    high(Z0 + t, x2T[:, t, :, :])
                    act.wait_ge(gap_done, nth("gap", b, t))
                    nc.scalar.activation(route[:, 17:18], route[:, 16:17], ACT.Exp).then_inc(gap_exp, 1)

        @block.vector
        def _(dve):
            for name in ("khat", "kvbd", "qhat", "mean", "num", "x2", "mean2", "logit_copied", "gap", "egate", "acc"):
                dve.sem_inc(SEMS[name], PER[name])
            for n in range(5):
                for k in range(KT):
                    dve.wait_ge(hi_done, n * KT + k + 1)
                    nc.vector.tensor_tensor(w_lo[:, n, k, :], tp[(n * KT + k) % 2][:, :, :].rearrange("p a c -> p (a c)"),
                                            w_hi[:, n, k, :].bitcast(F32), ALU.subtract).then_inc(lo_done, 1)
            dve.wait_ge(small_loaded, 80)
            dve.wait_ge(consts, 1)
            nc.vector.tensor_copy(bias[:, :], bias_raw[:, :]).then_inc(dve_step, 1)
            dve.wait_ge(dve_step, 1)
            nc.vector.tensor_tensor(bias[32:64, :], bias_raw[32:64, :], bias[32:64, :].bitcast(F32),
                                    ALU.subtract).then_inc(consts, 1)

            STEPS_Q = 2 * TT + 2 * TT + 2 * TT + 8 * TT
            base = 1

            with dve.Fori(0, B) as b:
                count = [0]

                def link(ins):
                    count[0] += 1
                    ins.then_inc(dve_step, 1)
                    dve.wait_ge(dve_step, b * STEPS_Q + base + count[0])

                def low(u, dst, hi):
                    dve.wait_ge(hi_done, nth("hi", b, u))
                    nc.vector.tensor_tensor(dst, tp[u % 2][:, :, :], hi.bitcast(F32), ALU.subtract).then_inc(lo_done, 1)

                def low_c(i):
                    low(i, ctxT_lo[:, i % 2, :, :], ctxT_hi[:, i % 2, :, :])

                def low_x(t):
                    low(X0 + t, xT_lo[:, :, t * P:(t + 1) * P], xT_hi[:, :, t * P:(t + 1) * P])

                def stats_x(t):
                    if t == 0:
                        dve.wait_ge(x_loaded, b * 16 + 16)
                        dve.wait_ge(xn_done, nth("xn", b, -1))
                    link(nc.vector.bn_stats(stats[:, :], x_raw[:, t, :]))
                    dve.sem_inc(dve_passed, 1)
                    agg = nc.vector.bn_aggr(mv[:, 0, t, :], stats[:, :])
                    if t < TT - 1:
                        link(agg)
                    else:
                        agg.then_inc(mean_done, 1)

                for i in range(ST):
                    if i == 0:
                        low_c(0)
                    if i + 1 < ST:
                        low_c(i + 1)
                    if i == ST - 2:
                        low_x(0)
                    if i == ST - 1:
                        low_x(1)
                        low_x(2)
                    dve.wait_ge(mink_done, nth("mink", b, i))
                    if i >= 2:
                        dve.wait_ge(kv_done, b * ST + i - 1)
                    nc.vector.scalar_tensor_tensor(khat[:, i % 2, :], pj[(2 * i) % 4][:, :], 1.0, expk[:, i % 2, :],
                                                   ALU.add, ALU.max).then_inc(khat_done, 1)
                    if i < TT:
                        stats_x(i)
                low_x(3)
                dve.wait_ge(kv_done, b * ST + ST)
                for h in range(2):
                    m = mask[:, :].rearrange("p (a c) -> p a c", a=1).broadcast_to((P, 2, CW))
                    last = nc.vector.tensor_tensor(kvbd[:, 2 * h:2 * h + 2, :], kvp[h][:, :, :], m, ALU.mult)
                last.then_inc(kvbd_done, 1)
                for g in range(G):
                    dve.wait_ge(minq_done, nth("minq", b, g))
                    nc.vector.scalar_tensor_tensor(qhat[:, g, :], pj[(FIRST_Q + g) % 4][:, :], 1.0, expq[:, g % 2, :],
                                                   ALU.add, ALU.max).then_inc(qhat_done, 1)

                def attend(t):
                    dve.wait_ge(at_done, nth("at", b, t))
                    for h in range(2):
                        last = nc.vector.tensor_scalar(
                            den[:, t % 2, 8 * h:8 * h + 8].rearrange("p (g c) -> p g c", g=2),
                            pj[(FIRST_AT + 2 * t + h) % 4][:, 0:2 * CW].rearrange("p (g c) -> p g c", g=2)[:, :, P:CW],
                            ATTN_EPS, None, ALU.add)
                    link(last)
                    link(nc.vector.reciprocal(z[:, t % 2, :], den[:, t % 2, :]))
                    dve.wait_ge(ag_done, nth("ag", b, t - 2))
                    for h in range(2):
                        for g in range(2):
                            zz = z[:, t % 2, 8 * h + 4 * g:8 * h + 4 * g + 4].rearrange("p (c a) -> p c a", a=1)
                            last = nc.vector.tensor_tensor(
                                num[:, t % 2, (2 * h + g) * P:(2 * h + g + 1) * P].rearrange("p (c e) -> p c e", c=HG),
                                pj[(FIRST_AT + 2 * t + h) % 4][:, g * CW:g * CW + P].rearrange("p (c e) -> p c e", c=HG),
                                zz.broadcast_to((P, HG, HD)), ALU.mult)
                    last.then_inc(num_done, 1)

                def low_a(t):
                    low(AG0 + t, agT_lo[:, t % 2, :, :], agT_hi[:, t % 2, :, :])

                def residual(t):
                    dve.wait_ge(wo_done, nth("wo", b, t))
                    nc.vector.tensor_tensor(x2[:, t, :], pj[(FIRST_WO + t) % 4][:, :], x_raw[:, t, :], ALU.add).then_inc(x2_done, 1)
                    dve.wait_ge(x2_done, nth("x2", b, t))
                    link(nc.vector.bn_stats(stats[:, :], x2[:, t, :]))
                    dve.sem_inc(dve_passed, 1)
                    nc.vector.bn_aggr(mv[:, 1, t, :], stats[:, :]).then_inc(mean2_done, 1)
                    dve.wait_ge(mean2_done, nth("mean2", b, t))

                attend(0)
                attend(1)
                low_a(0)
                attend(2)
                low_a(1)
                attend(3)
                residual(0)
                low_a(2)
                residual(1)
                low_a(3)
                residual(2)
                residual(3)

                def router(t):
                    lg, top, gap, ex = route[:, 0:8], route[:, 8:16], route[:, 16:17], route[:, 17:18]
                    tot, w1, w2, idf, one = route[:, 18:19], route[:, 19:20], route[:, 20:21], route[:, 24:32], route[:, 32:40]
                    dve.wait_ge(logit_done, nth("logit", b, t))
                    nc.vector.tensor_copy(lg, pj[(FIRST_LOGIT + t) % 4][:, 0:E]).then_inc(logit_copied, 1)
                    dve.wait_ge(logit_copied, nth("logit_copied", b, t))
                    dve.sem_inc(dve_passed, 1)
                    link(nc.vector.max(top, lg))
                    nc.vector.tensor_tensor(gap, top[:, 1:2], top[:, 0:1], ALU.subtract).then_inc(gap_done, 1)
                    link(nc.vector.max_index(routei[:, :], top, lg))
                    link(nc.vector.tensor_copy(idf, routei[:, :]))
                    dve.wait_ge(gap_exp, nth("gap_exp", b, t))
                    link(nc.vector.tensor_scalar(tot, ex, 1.0, None, ALU.add))
                    link(nc.vector.reciprocal(w1, tot))
                    link(nc.vector.tensor_tensor(w2, ex, w1, ALU.mult))
                    link(nc.vector.tensor_scalar(one, iota8[:, :], idf[:, 1:2], w2, ALU.is_equal, ALU.mult))
                    link(nc.vector.tensor_scalar(egate[:, t, :], iota8[:, :], idf[:, 0:1], w1, ALU.is_equal, ALU.mult))
                    nc.vector.tensor_tensor(egate[:, t, :], egate[:, t, :], one, ALU.add).then_inc(egate_done, 1)
                    dve.wait_ge(egate_done, nth("egate", b, t))

                for t in range(TT):
                    dve.wait_ge(lo_done, nth("lo", b, Z0 + t - 1))
                    dve.wait_ge(hi_done, nth("hi", b, Z0 + t))
                    dve.sem_inc(lo_done, 1)
                    router(t)
                for e in range(E):
                    for t in range(TT):
                        n = e * TT + t
                        dve.wait_ge(moe_done, nth("moe", b, n))
                        if e == 0:
                            dve.wait_ge(x2n_done, nth("x2n", b, t))
                        else:
                            dve.wait_ge(acc_done, nth("acc", b, n - TT))
                        nc.vector.scalar_tensor_tensor(x2[:, t, :], pj[(FIRST_MOE + n) % 4][:, :], egate[:, t, e:e + 1],
                                                       x2[:, t, :], ALU.mult, ALU.add).then_inc(acc_done, 1)
                dve.wait_ge(stored, b * 16 * TT + 16 * TT)
                assert count[0] <= STEPS_Q
                for _ in range(STEPS_Q - count[0]):
                    dve.sem_inc(dve_step, 1)

        @block.tensor
        def _(pe):
            for name in ("k", "v", "q", "g", "at", "wo", "logit", "moe"):
                pe.sem_inc(SEMS[name], PER[name])
            pe.wait_ge(consts, 6)
            for n in range(5):
                pe.wait_ge(w_loaded[n % 2], 16 * (n // 2 + 1))
                for k in range(KT):
                    u = n * KT + k
                    if u >= 2:
                        pe.wait_ge(lo_done, u - 1)
                    for a in range(4):
                        last = nc.tensor.transpose(tp[u % 2][:, a, :], wraw[:, n % 2, a, k * P:(k + 1) * P], ident[:, :])
                    last.then_inc(turned, 1)
            pe.wait_ge(consts, 7)

            with pe.Fori(0, B) as b:
                def free(n):
                    name, i = USES[n - 4]
                    pe.wait_ge(SEMS[name], nth(name, b, i if n >= 4 else i - PER[name]))

                def turn(u, src):
                    pe.wait_ge(lo_done, nth("lo", b, u - 2))
                    for k in range(KT):
                        last = nc.tensor.transpose(tp[u % 2][:, k, :], src[:, k * P:(k + 1) * P], ident[:, :])
                    last.then_inc(turned, 1)

                def three(out_ap, s_hi, s_lo, m_hi, m_lo, bias_row=None):
                    for k in range(KT):
                        nc.tensor.matmul(out_ap, s_hi(k), m_hi(k), start=(k == 0), stop=False)
                        nc.tensor.matmul(out_ap, s_hi(k), m_lo(k), start=False, stop=False)
                        last = nc.tensor.matmul(out_ap, s_lo(k), m_hi(k), start=False, stop=(k == KT - 1 and bias_row is None))
                    if bias_row is not None:
                        last = nc.tensor.matmul(out_ap, pick[:, bias_row, :], bias[:, :], start=False, stop=True)
                    return last

                def turn_c(i):
                    pe.wait_ge(ctx_loaded[(i // 2) % 2], b * 32 + 16 * (i // 4 + 1))
                    turn(i, ctx_raw[:, (i // 2) % 2, i % 2, :])

                def turn_x(t):
                    pe.wait_ge(xn_done, nth("xn", b, t))
                    turn(X0 + t, xn[:, t % 2, :])

                def kv_project(i):
                    pe.wait_ge(lo_done, nth("lo", b, i))
                    for j, (w, done) in enumerate(((WK, k_done), (WV, v_done))):
                        free(2 * i + j)
                        three(pj[(2 * i + j) % 4][:, :], lambda k: ctxT_hi[:, i % 2, k, :], lambda k: ctxT_lo[:, i % 2, k, :],
                              lambda k: w_hi[:, w, k, :], lambda k: w_lo[:, w, k, :]).then_inc(done, 1)

                def kv_sum(i):
                    pe.wait_ge(khat_done, nth("khat", b, i))
                    pe.wait_ge(v_copied, nth("v_copied", b, i))
                    if i == 0:
                        pe.wait_ge(kvbd_done, nth("kvbd", b, -1))
                    for g in range(G):
                        last = nc.tensor.matmul(kvp[g // 2][:, g % 2, :], khat[:, i % 2, g * P:(g + 1) * P], vones[:, i % 2, g, :],
                                                start=(i == 0 and g % 2 == 0), stop=(i == ST - 1), skip_group_check=True)
                    last.then_inc(kv_done, 1)

                for i in range(ST):
                    if i == 0:
                        turn_c(0)
                    if i + 1 < ST:
                        turn_c(i + 1)
                    if i == ST - 2:
                        turn_x(0)
                    if i == ST - 1:
                        turn_x(1)
                        turn_x(2)
                    kv_project(i)
                    if i >= 1:
                        kv_sum(i - 1)
                turn_x(3)
                kv_sum(ST - 1)
                pe.wait_ge(lo_done, nth("lo", b, X0 + TT - 1))
                for g in range(G):
                    free(FIRST_Q + g)
                    three(pj[(FIRST_Q + g) % 4][:, :], lambda k: w_hi[:, WQ, k, g * P:(g + 1) * P], lambda k: w_lo[:, WQ, k, g * P:(g + 1) * P],
                          lambda k: xT_hi[:, k, :], lambda k: xT_lo[:, k, :]).then_inc(q_done, 1)
                for t in range(TT):
                    free(FIRST_G + t)
                    three(pj[(FIRST_G + t) % 4][:, :], lambda k: xT_hi[:, k, t * P:(t + 1) * P], lambda k: xT_lo[:, k, t * P:(t + 1) * P],
                          lambda k: w_hi[:, WG, k, :], lambda k: w_lo[:, WG, k, :], bias_row=0).then_inc(g_done, 1)

                def attend(t):
                    if t == 0:
                        pe.wait_ge(kvbd_done, nth("kvbd", b, 0))
                        pe.wait_ge(qhat_done, nth("qhat", b, G - 1))
                    for h in range(2):
                        free(FIRST_AT + 2 * t + h)
                        for g in range(2 * h, 2 * h + 2):
                            last = nc.tensor.matmul(pj[(FIRST_AT + 2 * t + h) % 4][:, (g % 2) * CW:(g % 2 + 1) * CW],
                                                    qhat[:, g, t * P:(t + 1) * P], kvbd[:, g, :], start=True, stop=True,
                                                    skip_group_check=True)
                    last.then_inc(at_done, 1)

                def turn_a(t):
                    pe.wait_ge(ag_done, nth("ag", b, t))
                    turn(AG0 + t, ag[:, t % 2, :])

                def project_out(t):
                    pe.wait_ge(lo_done, nth("lo", b, AG0 + t))
                    free(FIRST_WO + t)
                    three(pj[(FIRST_WO + t) % 4][:, :], lambda k: agT_hi[:, t % 2, k, :], lambda k: agT_lo[:, t % 2, k, :],
                          lambda k: w_hi[:, WO, k, :], lambda k: w_lo[:, WO, k, :]).then_inc(wo_done, 1)

                attend(0)
                attend(1)
                turn_a(0)
                attend(2)
                turn_a(1)
                attend(3)
                project_out(0)
                turn_a(2)
                project_out(1)
                turn_a(3)
                project_out(2)
                project_out(3)
                for t in range(TT):
                    pe.wait_ge(x2n_done, nth("x2n", b, t))
                    turn(Z0 + t, x2n[:, t % 2, :])
                    pe.wait_ge(hi_done, nth("hi", b, Z0 + t))
                    free(FIRST_LOGIT + t)
                    for k in range(KT):
                        last = nc.tensor.matmul(pj[(FIRST_LOGIT + t) % 4][:, 0:E], x2T[:, t, k, :], wr_sb[:, k, :],
                                                start=(k == 0), stop=(k == KT - 1))
                    last.then_inc(logit_done, 1)
                for e in range(E):
                    pe.wait_ge(we_loaded[e % 2], b * 16 * (E // 2) + 16 * (e // 2 + 1))
                    for t in range(TT):
                        n = e * TT + t
                        free(FIRST_MOE + n)
                        for k in range(KT):
                            nc.tensor.matmul(pj[(FIRST_MOE + n) % 4][:, :], x2T[:, t, k, :], wraw[:, e % 2, k, :], start=(k == 0), stop=False)
                        nc.tensor.matmul(pj[(FIRST_MOE + n) % 4][:, :], pick[:, 1 + e, :], bias[:, :], start=False, stop=True).then_inc(moe_done, 1)


_INS = ["x", "ctx_2048", "L0_xattn_Wq", "L0_xattn_Wg", "L0_xattn_bg", "L0_xattn_Wkv", "L0_xattn_Wo",
        "L0_ffn_Wr", "L0_ffn_We", "L0_ffn_be"]
_OUTS = [((4, 512, 512), "float32")]


def kernel(**inputs):
    import numpy as _np
    import concourse.bacc as _bacc
    from concourse import mybir as _mybir
    from concourse.bass_utils import run_bass_kernel_spmd as _run

    nc = _bacc.Bacc("TRN2", target_bir_lowering=False, num_devices=1)
    arrays, args = {}, []
    for name in _INS:
        a = _np.ascontiguousarray(inputs[name])
        arrays[f"in_{name}_dram"] = a
        args.append(nc.dram_tensor(f"in_{name}_dram", a.shape, _mybir.dt.from_np(a.dtype), kind="ExternalInput").ap())
    for i, (shape, dtype) in enumerate(_OUTS):
        dt = _mybir.dt.from_np(_np.dtype(dtype))
        args.append(nc.dram_tensor(f"out_{i}_dram", shape, dt, kind="ExternalOutput").ap())
    xattn_moe_kernel(nc, *args)
    r = _run(nc, [arrays], core_ids=[0])
    got = tuple(r.results[0][f"out_{i}_dram"] for i in range(len(_OUTS)))
    return got[0]
```

```python
from contextlib import ExitStack

import concourse.bass as bass
from concourse import mybir

F32 = mybir.dt.float32
F32R = mybir.dt.float32r
U32 = mybir.dt.uint32
I32 = mybir.dt.int32
ALU = mybir.AluOpType
ACT = mybir.ActivationFunctionType
AX_X = mybir.AxisListType.X

P = 128
HEADS = 16
ATTN_EPS = 1e-6
NORM_EPS = 1e-5


def xattn_moe_kernel(nc, x, ctx_in, wq, wg, bg, wkv, wo, wr, we, be, out):
    B, L, D = x.shape
    S = ctx_in.shape[1]
    E = we.shape[0]
    KT = D // P
    ST = S // P
    TT = L // P
    G = D // P
    HG = HEADS // G
    HD = D // HEADS
    CW = P + HG
    assert L == D == 512 and ST == 8 and TT == KT == 4 and E == 8

    GROUP_TILES = ((B - 1) * TT, TT)
    ROWS = [n * P + P for n in GROUP_TILES]
    TILES = [2 * n + E - 1 for n in GROUP_TILES]
    FIRST = [0, TILES[0]]
    M_ALL = sum(TILES)
    NQ = B * TT

    xs_dram = [nc.dram_tensor(f"xs{g}", [E * ROWS[g], D], F32, kind="Internal").ap() for g in range(2)]
    y_dram = [nc.dram_tensor(f"y{g}", [TILES[g] * P, D], F32, kind="Internal").ap() for g in range(2)]
    x2_dram = nc.dram_tensor("x2_rows", [B * L, D], F32, kind="Internal").ap()
    out_rows = out.rearrange("b l d -> (b l) d")

    with ExitStack() as stack:
        def sb(name, shape, dt=F32):
            return stack.enter_context(nc.sbuf_tensor(name, shape, dt))

        def sem(name):
            return stack.enter_context(nc.semaphore(name))

        R = sb("R", [P, 2 * E, KT, D], F32R)
        WK, WV, WQ, WG, WO = range(5)

        def w_hi(n):
            return R[:, 2 + 2 * n, :, :]

        def w_lo(n):
            return R[:, 3 + 2 * n, :, :]

        xT_hi, xT_lo = R[:, 12, :, :], R[:, 13, :, :]
        ctxT_hi = R[:, 14, 0:2, :].rearrange("p s (k c) -> p s k c", k=KT)
        ctxT_lo = R[:, 14, 2:4, :].rearrange("p s (k c) -> p s k c", k=KT)
        agT_hi = R[:, 15, 0:2, :].rearrange("p s (k c) -> p s k c", k=KT)
        agT_lo = R[:, 15, 2:4, :].rearrange("p s (k c) -> p s k c", k=KT)
        aux = sb("aux", [P, 4, D], F32R)
        bias = aux[0:64, 0, :]
        pick = aux[0:64, 1, 0:P]
        xsT_hi = aux[:, 0:2, :].rearrange("p s (k c) -> p s k c", k=KT)
        xsT_lo = aux[:, 2:4, :].rearrange("p s (k c) -> p s k c", k=KT)

        wraw = sb("wraw", [P, 2, KT, D])
        x_raw = wraw[:, 1, :, :]
        BUF = 4 * D + G * 2 * CW + 2 * D
        buf = sb("buf", [P, BUF])
        ctx_raw = buf[:, 0:4 * D].rearrange("p (s t d) -> p s t d", s=2, t=2)
        vones = buf[:, 4 * D:4 * D + 2 * G * CW].rearrange("p (s g c) -> p s g c", s=2, g=G)
        expk = buf[:, 4 * D + 2 * G * CW:BUF].rearrange("p (s d) -> p s d", s=2)
        expq = expk
        be_all = buf[:, 0:E * D].rearrange("p (e d) -> p e d", e=E)
        khat = sb("khat", [P, 2, D])
        xs_raw = khat
        kvbd = sb("kvbd", [P, G, CW])
        zeros = sb("zeros", [P, D])
        bias_raw = zeros[0:64, :]
        y_sb = [kvbd[:, :, :].rearrange("p g c -> p (g c)")[:, 0:D], zeros[:, :]]
        num = sb("num", [P, 2, D])
        xn = num
        qhat = sb("qhat", [P, G, L])
        x2T = qhat[:, :, :].rearrange("p t (k c) -> p t k c", k=KT)
        gate = sb("gate", [P, TT, D])
        x2 = gate
        x2n = sb("x2n", [P, 2, D])
        x2r = qhat[:, 0:2, :]
        yg = gate

        ident = sb("ident", [P, P])
        before = sb("before", [P, P])
        ones = sb("ones", [P, P])
        mask = sb("mask", [P, CW])
        wr_sb = sb("wr_sb", [P, KT, E])
        iota8 = sb("iota8", [P, E])
        iota_t = sb("iota_t", [P, max(TILES)])
        steps = sb("steps", [P, max(GROUP_TILES)])
        below = sb("below", [P, E, E])
        mhalf = sb("mhalf", [P, TT])
        stats = sb("stats", [P, 6])
        mv = sb("mv", [P, 2, TT, 2])
        rstd = sb("rstd", [P, 2, TT])
        den = sb("den", [P, 2, HEADS])
        z = sb("z", [P, 2, HEADS])
        lg = sb("lg", [P, E])
        top = sb("top", [P, E])
        gap = sb("gap", [P, 1])
        egap = sb("egap", [P, 1])
        total = sb("total", [P, 1])
        idx8 = sb("idx8", [P, E], U32)
        idf = sb("idf", [P, TT, E])
        both = sb("both", [P, 2, E])
        members = sb("members", [P, 2, E])
        w_top = sb("w_top", [P, 2])
        pos = sb("pos", [P, E])
        prod = sb("prod", [P, 2, E])
        rank_t = sb("rank_t", [P, 2])
        run = sb("run", [P, 2, E])
        onehot = sb("onehot", [P, NQ, 2, E])
        rank = sb("rank", [P, NQ, 2])
        wts = sb("wts", [P, NQ, 2])
        yslot = sb("yslot", [P, NQ, 2])
        xidx = sb("xidx", [P, TT, 2], U32)
        gidx = sb("gidx", [P, 2, 2], U32)
        nt = sb("nt", [P, 1 + E])
        tb = sb("tb", [P, E])
        last_t = sb("last_t", [P, 1])
        tile_t = sb("tile_t", [P, max(TILES)])
        tile_e = sb("tile_e", [P, max(TILES)])
        tile_b = sb("tile_b", [P, max(TILES)])
        tile_expert = sb("tile_expert", [P, M_ALL], I32)
        tile_row = sb("tile_row", [P, M_ALL], I32)
        pad_row = sb("pad_row", [P, 2, E], I32)

        tp = [stack.enter_context(nc.psum_tensor(f"tp{i}", [P, KT, P], F32)) for i in range(2)]
        pj = [stack.enter_context(nc.psum_tensor(f"pj{i}", [P, D], F32)) for i in range(4)]
        kvb = [stack.enter_context(nc.psum_tensor(f"kvb{i}", [P, D], F32)) for i in range(2)]
        late_z = [a[:, :].rearrange("p (k c) -> p k c", k=KT) for a in kvb]
        kvp = [a[:, 0:2 * CW].rearrange("p (g c) -> p g c", g=2) for a in kvb]

        w_loaded = [sem(f"w_loaded{i}") for i in range(2)]
        small_loaded, x_loaded, be_loaded = sem("small_loaded"), sem("x_loaded"), sem("be_loaded")
        ctx_loaded = [sem(f"ctx_loaded{i}") for i in range(2)]
        x2_stored = sem("x2_stored")
        scattered = [sem(f"scattered{i}") for i in range(2)]
        padded = [sem(f"padded{g}") for g in range(2)]
        xs_loaded = [sem(f"xs_loaded{i}") for i in range(2)]
        y_stored = [sem(f"y_stored{i}") for i in range(2)]
        gathered = [sem(f"gathered{i}") for i in range(2)]
        x2r_loaded = [sem(f"x2r_loaded{i}") for i in range(2)]
        out_stored = [sem(f"out_stored{i}") for i in range(2)]
        e0_loaded = sem("e0_loaded")
        e_loaded = [sem(f"e_loaded{i}") for i in range(2)]
        consts, zeroed = sem("consts"), sem("zeroed")
        bias_cut = sem("bias_cut")
        w_turned, w_high, w_low = sem("w_turned"), sem("w_high"), sem("w_low")
        e0_high, e_high, we_ready = sem("e0_high"), sem("e_high"), sem("we_ready")
        planned = sem("planned")
        half_combined = sem("half_combined")
        gidx_done, combined = sem("gidx_done"), sem("combined")
        dve_step, pool_step = sem("dve_step"), sem("pool_step")
        dve_passed, pool_passed = sem("dve_passed"), sem("pool_passed")

        PER = {
            "t_c": ST, "h_c": ST, "l_c": ST, "t_x": TT, "h_x": TT, "l_x": TT, "t_a": TT, "h_a": TT, "l_a": TT,
            "t_z": TT, "h_z": TT, "k": ST, "v": ST, "kv": ST, "q": G, "g": TT, "at": TT, "wo": TT,
            "logit": TT, "prefix": TT, "expk": ST, "mink": ST, "khat": ST, "v_copied": ST, "kvbd": 1,
            "expq": G, "minq": G, "qhat": G, "gate": TT, "mean": 1, "xn": TT, "num": TT, "ag": TT,
            "x2": TT, "mean2": TT, "x2n": TT, "logit_copied": TT, "gap": TT, "egap": TT, "picked": TT,
            "ranked": TT, "slot": TT,
        }
        SEMS = {name: sem(name) for name in PER}

        def nth(name, b, i):
            return (b + 1) * PER[name] + i + 1

        MOE = {name: sem(name) for name in ("t_m", "h_m", "l_m", "m_done", "y_copied")}

        def mth(m):
            return m + 3

        KEYS = []
        turns = {0: "c0 c1", 1: "c2 z0", 2: "c3 z1", 3: "c4", 4: "c5 z2", 5: "c6 z3", 6: "c7 x0", 7: "x1 x2"}
        logits = {1: 0, 2: 1, 4: 2, 5: 3}
        prefixes = {2: 0, 3: 1, 5: 2, 6: 3}
        for i in range(ST):
            KEYS += [("T", s[0], int(s[1])) for s in turns[i].split()] + [("P", "", i)]
            KEYS += [("L", "", logits[i])] if i in logits else []
            KEYS += [("K", "", prefixes[i])] if i in prefixes else []
            KEYS += [("KV", "", i - 1)] if i >= 1 else []
        KEYS += [("T", "x", 3), ("KV", "", ST - 1)]
        QUERIES = [("Q", "", g) for g in range(G)] + [("G", "", t) for t in range(TT)]
        QUERIES += [("A", "", 0), ("A", "", 1), ("T", "a", 0), ("A", "", 2), ("T", "a", 1), ("A", "", 3), ("O", "", 0),
                    ("T", "a", 2), ("O", "", 1), ("T", "a", 3), ("O", "", 2), ("O", "", 3)]

        TP_USES, PJ_USES = [], []
        for step, kind, i in KEYS + QUERIES:
            if step == "T":
                TP_USES.append(("h_z" if kind == "z" else "l_" + kind, i))
            else:
                PJ_USES += {"P": [("khat", i), ("v_copied", i)], "L": [("logit_copied", i)], "K": [("ranked", i)],
                            "KV": [], "Q": [("qhat", i)], "G": [("gate", i)], "A": [("num", i)] * 2, "O": [("x2", i)]}[step]
        assert len(TP_USES) % 2 == 0 and len(PJ_USES) % 4 == 0
        OF_BATCH_BEFORE = ("h_z", "logit_copied", "ranked")

        def tp_bank(name, i):
            return tp[TP_USES.index((name, i)) % 2]

        def halves(kind, i):
            if kind == "x":
                return xT_hi[:, :, i * P:(i + 1) * P], xT_lo[:, :, i * P:(i + 1) * P]
            hi, lo = (ctxT_hi, ctxT_lo) if kind == "c" else (agT_hi, agT_lo)
            return hi[:, i % 2, :, :], lo[:, i % 2, :, :]

        def pj_bank(name, i, second=0):
            return pj[(PJ_USES.index((name, i)) + second) % 4]

        def tiles(m):
            return [("T", "m", m + 1), ("M", "", m)]

        START = [("T", "m", 0)] + tiles(0) + tiles(1) + [("T", "z", 0), ("T", "z", 1)] + tiles(2)
        START += [("L", "", 0), ("L", "", 1), ("T", "z", 2), ("T", "z", 3)] + tiles(3)
        START += [("K", "", 0), ("K", "", 1), ("L", "", 2), ("L", "", 3)] + tiles(4) + [("K", "", 2), ("K", "", 3)]
        LOOP1 = 5
        N_COMB = GROUP_TILES[0]
        LOOP2 = M_ALL - N_COMB
        assert (FIRST[1] - LOOP1) % 2 == 0 and N_COMB % 2 == 0 and LOOP2 > FIRST[1]

        def group_of(m):
            return 0 if m < FIRST[1] else 1

        block = stack.enter_context(nc.Block())

        @block.sync
        def _(sp):
            srcs = [wkv[0:D, :], wkv[D:2 * D, :], wq, wg, wo]
            for n, src in enumerate(srcs):
                if n >= 2:
                    sp.wait_ge(w_turned, KT * (n - 1))
                sp.dma_start(wraw[:, n % 2, :, :], src.rearrange("(a p) d -> p a d", p=P)).then_inc(w_loaded[n % 2], 16)
                if n == 0:
                    sp.dma_start(wr_sb[:, :, :], wr.rearrange("(k p) e -> p k e", p=P)).then_inc(small_loaded, 16)
                    sp.wait_ge(zeroed, 1)
                    for row in (0, 32):
                        sp.dma_start(bias_raw[row:row + 1, :], bg.rearrange("(a d) -> a d", a=1)).then_inc(small_loaded, 16)
            sp.wait_ge(w_turned, KT * 4)
            sp.dma_start(wraw[:, 1, :, :], we[0, :, :].rearrange("(k p) f -> p k f", p=P)).then_inc(e0_loaded, 16)

            def ctx_pair(b, j):
                sp.wait_ge(SEMS["t_c"], nth("t_c", b, 2 * j - 3))
                sp.dma_start(ctx_raw[:, j % 2, :, :],
                             ctx_in[b, 2 * j * P:(2 * j + 2) * P, :].rearrange("(t p) d -> p t d", p=P)).then_inc(ctx_loaded[j % 2], 16)

            def store_x2(b):
                sp.wait_ge(SEMS["x2"], nth("x2", b, TT - 1))
                sp.dma_start(x2_dram[bass.ds(b * L, L), :].rearrange("(t p) d -> p t d", p=P), x2[:, :, :]).then_inc(x2_stored, 16)

            def load_x(b):
                sp.dma_start(x_raw, x[b, :, :].rearrange("(t p) d -> p t d", p=P)).then_inc(x_loaded, 16)

            ctx_pair(0, 0)
            ctx_pair(0, 1)
            sp.wait_ge(we_ready, 1)
            load_x(0)
            ctx_pair(0, 2)
            ctx_pair(0, 3)
            with sp.Fori(0, B - 1) as b:
                ctx_pair(b + 1, 0)
                ctx_pair(b + 1, 1)
                store_x2(b)
                load_x(b + 1)
                ctx_pair(b + 1, 2)
                ctx_pair(b + 1, 3)

            def pad(g, src):
                with sp.Fori(0, E) as e:
                    row = sp.value_load(pad_row[0:1, g, bass.ds(e, 1)], min_val=0, max_val=E * ROWS[g] - P)
                    sp.dma_start(xs_dram[g][bass.ds(row, P), :], src).then_inc(padded[g], 16)

            def load_tile(g, m, slot):
                row = sp.value_load(tile_row[0:1, bass.ds(m, 1)], min_val=0, max_val=E * ROWS[g] - P)
                sp.wait_ge(MOE["t_m"], mth(m - 2))
                sp.dma_start(xs_raw[:, slot, :], xs_dram[g][bass.ds(row, P), :]).then_inc(xs_loaded[slot], 16)

            def load_x2r(c, slot, n):
                sp.wait_ge(out_stored[slot], 16 * n + 16)
                sp.dma_start(x2r[:, slot, :], x2_dram[bass.ds(c * P, P), :]).then_inc(x2r_loaded[slot], 16)

            sp.wait_ge(planned, 1)
            pad(0, zeros[:, :])
            sp.wait_ge(padded[0], 16 * E)
            for s in range(2):
                sp.wait_ge(scattered[s], 64 * (B - 1))
            load_tile(0, 0, 0)
            load_tile(0, 1, 1)
            sp.wait_ge(SEMS["qhat"], nth("qhat", B - 1, G - 1))
            for e in range(E):
                sp.dma_start(be_all[:, e, :], be[e:e + 1, :].broadcast_to((P, D))).then_inc(be_loaded, 16)
            store_x2(B - 1)
            load_tile(0, 2, 0)
            with sp.Fori(0, (FIRST[1] - 3) // 2) as h:
                load_tile(0, 2 * h + 3, 1)
                load_tile(0, 2 * h + 4, 0)
            sp.wait_ge(zeroed, 3)
            pad(1, x2n[:, 0, :])
            sp.wait_ge(padded[1], 16 * E)
            for m in range(FIRST[1], LOOP2):
                load_tile(1, m, m % 2)
            sp.wait_ge(x2_stored, 16 * (B + 1))
            with sp.Fori(0, N_COMB // 2) as h:
                for s in range(2):
                    load_tile(1, 2 * h + LOOP2 + s, (LOOP2 + s) % 2)
                    load_x2r(2 * h + s, s, h)
            for c in range(N_COMB, NQ):
                load_x2r(c, c % 2, c // 2)

        @block.gpsimd
        def _(pool):
            for name in ("mink", "minq", "xn", "x2n", "ag"):
                pool.sem_inc(SEMS[name], PER[name])
            for s in range(2):
                pool.sem_inc(out_stored[s], 16)
                pool.sem_inc(y_stored[s], 16)
            pool.sem_inc(x2_stored, 16)
            n_step = [0, 0, 0]

            def link(ins):
                n_step[0] += 1
                ins.then_inc(pool_step, 1)
                pool.wait_ge(pool_step, n_step[2] * n_step[1] + n_step[0])

            def passed():
                pool.sem_inc(pool_passed, 1)

            nc.gpsimd.memset(zeros[:, :], 0.0).then_inc(zeroed, 1)
            link(nc.gpsimd.memset(ident[:, :], 0.0))
            link(nc.gpsimd.affine_select(out=ident[:, :], in_=ident[:, :], compare_op=ALU.not_equal, fill=1.0,
                                         base=0, pattern=[[-1, P]], channel_multiplier=1))
            nc.gpsimd.memset(ones[:, :], 1.0).then_inc(consts, 1)
            nc.gpsimd.memset(vones[:, :, :, P:CW], 1.0).then_inc(consts, 1)
            nc.gpsimd.memset(mhalf[:, :], -0.5).then_inc(consts, 1)
            nc.gpsimd.memset(nt[:, 0:1], 0.0).then_inc(consts, 1)
            nc.gpsimd.memset(run[:, :, :], 0.0).then_inc(consts, 1)
            nc.gpsimd.iota(iota8[:, :], pattern=[[1, E]], base=0, channel_multiplier=0,
                           allow_small_or_imprecise_dtypes=True).then_inc(consts, 1)
            nc.gpsimd.iota(iota_t[:, :], pattern=[[1, max(TILES)]], base=0, channel_multiplier=0,
                           allow_small_or_imprecise_dtypes=True).then_inc(consts, 1)
            nc.gpsimd.iota(steps[:, :], pattern=[[P, max(GROUP_TILES)]], base=0, channel_multiplier=0,
                           allow_small_or_imprecise_dtypes=True).then_inc(consts, 1)
            link(nc.gpsimd.memset(mask[:, :], 1.0))
            m4 = mask[:, 0:P].rearrange("p (h e) -> p h e", h=HG)
            for ap, pat in ((m4, [[-HD, HG], [0, HD]]), (mask[:, P:CW], [[-HD, HG]])):
                link(nc.gpsimd.affine_select(out=ap, in_=ap, compare_op=ALU.is_ge, fill=0.0, base=0,
                                             pattern=pat, channel_multiplier=1))
                link(nc.gpsimd.affine_select(out=ap, in_=ap, compare_op=ALU.is_ge, fill=0.0, base=HD - 1,
                                             pattern=[[-s, c] for s, c in pat], channel_multiplier=-1))
            link(nc.gpsimd.memset(before[:, :], 0.0))
            link(nc.gpsimd.affine_select(out=before[:, :], in_=before[:, :], compare_op=ALU.is_ge, fill=1.0,
                                         base=0, pattern=[[-1, P]], channel_multiplier=1))
            link(nc.gpsimd.memset(below[:, :, :], 0.0))
            link(nc.gpsimd.affine_select(out=below[:, :, :], in_=below[:, :, :], compare_op=ALU.is_ge, fill=1.0,
                                         base=0, pattern=[[-1, E], [1, E]], channel_multiplier=0))
            link(nc.gpsimd.memset(gate[0:64, 0, 0:P], 0.0))
            for row in (0, 32):
                link(nc.gpsimd.affine_select(out=gate[0:64, 0, 0:P], in_=gate[0:64, 0, 0:P], compare_op=ALU.not_equal, fill=1.0,
                                             base=-row, pattern=[[0, P]], channel_multiplier=1))
            nc.gpsimd.tensor_copy(pick, gate[0:64, 0, 0:P]).then_inc(consts, 1)
            pool.wait_ge(bias_cut, 1)
            nc.gpsimd.memset(zeros[:, :], 0.0).then_inc(zeroed, 1)

            def rsqrt(k, t0, n):
                passed()
                link(nc.gpsimd.tensor_scalar(rstd[:, k, t0:t0 + n], mv[:, k, t0:t0 + n, 1], NORM_EPS, None, ALU.add))
                link(nc.gpsimd.tensor_tensor(rstd[:, k, t0:t0 + n], rstd[:, k, t0:t0 + n], mhalf[:, 0:n], ALU.pow))

            def norm_x(b, t):
                pool.wait_ge(SEMS["t_x" if t >= 2 else "t_a"], nth("t_x", b, t - 2) if t >= 2 else nth("t_a", b, -1))
                passed()
                nc.gpsimd.tensor_scalar(xn[:, t % 2, :], x_raw[:, t, :], mv[:, 0, t, 0:1], rstd[:, 0, t:t + 1],
                                        ALU.subtract, ALU.mult).then_inc(SEMS["xn"], 1)

            def norm_x2(b, t, dst, scatters=True):
                pool.wait_ge(SEMS["mean2"], nth("mean2", b, t))
                rsqrt(1, t, 1)
                if scatters:
                    if t >= 2:
                        pool.wait_ge(scattered[t % 2], b * 64 + 32)
                    pool.wait_ge(SEMS["t_z"], nth("t_z", b, t - 2))
                    passed()
                nc.gpsimd.tensor_scalar(dst, x2[:, t, :], mv[:, 1, t, 0:1], rstd[:, 1, t:t + 1],
                                        ALU.subtract, ALU.mult).then_inc(SEMS["x2n"], 1)

            def scatter(g, b, t, src):
                pool.wait_ge(SEMS["slot"], nth("slot", b, t))
                passed()
                for j in range(2):
                    nc.gpsimd.indirect_dma_start(out=xs_dram[g][:, :], out_offset=bass.IndirectOffsetOnAxis(ap=xidx[:, t, j:j + 1], axis=0),
                                                 in_=src, in_offset=None).then_inc(scattered[t % 2], 16)

            def min_k(b, i):
                pool.wait_ge(SEMS["expk"], nth("expk", b, i))
                passed()
                nc.gpsimd.tensor_scalar(expk[:, i % 2, :], expk[:, i % 2, :], 1.0, None, ALU.min).then_inc(SEMS["mink"], 1)

            def keys(b, before_):
                if before_ is not None:
                    norm_x2(before_, 0, x2n[:, 0, :])
                    norm_x2(before_, 1, x2n[:, 1, :])
                for i in range(ST):
                    min_k(b, i)
                    if before_ is not None:
                        if i == 2:
                            scatter(0, before_, 0, x2n[:, 0, :])
                        if i == 3:
                            scatter(0, before_, 1, x2n[:, 1, :])
                            norm_x2(before_, 2, x2n[:, 0, :])
                        if i == 4:
                            norm_x2(before_, 3, x2n[:, 1, :])
                    if i == 4:
                        pool.wait_ge(SEMS["mean"], nth("mean", b, 0))
                        rsqrt(0, 0, TT)
                        norm_x(b, 0)
                    if i == 5:
                        norm_x(b, 1)
                        norm_x(b, 2)
                        if before_ is not None:
                            scatter(0, before_, 2, x2n[:, 0, :])
                    if i == 6:
                        norm_x(b, 3)
                        if before_ is not None:
                            scatter(0, before_, 3, x2n[:, 1, :])
                if before_ is not None:
                    for s in range(2):
                        pool.wait_ge(scattered[s], before_ * 64 + 64)

            def queries(b):
                for g in range(G):
                    pool.wait_ge(SEMS["expq"], nth("expq", b, g))
                    passed()
                    nc.gpsimd.tensor_scalar(expq[:, g % 2, :], expq[:, g % 2, :], 1.0, None, ALU.min).then_inc(SEMS["minq"], 1)
                for t in range(TT):
                    pool.wait_ge(SEMS["num"], nth("num", b, t))
                    pool.wait_ge(SEMS["gate"], nth("gate", b, t))
                    nc.gpsimd.tensor_tensor(num[:, t % 2, :], num[:, t % 2, :], gate[:, t, :], ALU.mult).then_inc(SEMS["ag"], 1)

            keys(0, None)
            start, per = n_step[0], 2 + 2 * TT
            with pool.Fori(0, B - 1) as b:
                n_step[1:] = [per, b]
                queries(b)
                keys(b + 1, b)
                assert n_step[0] == start + per
            n_step[:] = [start + per * (B - 1), 0, 0]
            queries(B - 1)
            last = B - 1
            late = [x2n[:, 0, :], x2n[:, 1, :], num[:, 0, :], num[:, 1, :]]
            for t in range(TT):
                if t == 2:
                    pool.wait_ge(SEMS["t_a"], nth("t_a", last, TT - 1))
                norm_x2(last, t, late[t], scatters=False)

            pool.wait_ge(SEMS["wo"], nth("wo", last, TT - 1))
            pool.wait_ge(SEMS["x2"], nth("x2", last, TT - 1))
            for e in range(1, 3):
                pool.dma_start(wraw[:, (e + 1) % 2, :, :], we[e, :, :].rearrange("(k p) f -> p k f", p=P)).then_inc(e_loaded[(e + 1) % 2], 16)
            for e in range(1, E):
                s = (e + 1) % 2
                pool.wait_ge(e_loaded[s], 16 * ((e + 1) // 2))
                nc.gpsimd.tensor_copy(R[:, 2 * e, :, :], wraw[:, s, :, :]).then_inc(e_high, 1)
                pool.wait_ge(e_high, e)
                nc.gpsimd.tensor_tensor(R[:, 2 * e + 1, :, :], wraw[:, s, :, :], R[:, 2 * e, :, :].bitcast(F32),
                                        ALU.subtract).then_inc(we_ready, 1)
                if e + 2 < E:
                    pool.wait_ge(we_ready, e + 1)
                    pool.dma_start(wraw[:, s, :, :], we[e + 2, :, :].rearrange("(k p) f -> p k f", p=P)).then_inc(e_loaded[s], 16)
            for t in range(TT):
                scatter(1, last, t, late[t])
            for s in range(2):
                pool.wait_ge(scattered[s], 64 * B)
            nc.gpsimd.memset(x2n[:, 0, :], 0.0).then_inc(zeroed, 1)

            def gather(g, c, slot, n):
                pool.wait_ge(gidx_done, c + 1)
                passed()
                for j in range(2):
                    nc.gpsimd.indirect_dma_start(out=yg[:, 2 * slot + j, :], out_offset=None, in_=y_dram[g][:, :],
                                                 in_offset=bass.IndirectOffsetOnAxis(ap=gidx[:, slot, j:j + 1], axis=0)).then_inc(gathered[slot], 16)

            def y_ready(g):
                n = FIRST[g] + TILES[g]
                pool.wait_ge(y_stored[0], 16 + 16 * ((n + 1) // 2))
                pool.wait_ge(y_stored[1], 16 + 16 * (n // 2))

            pool.wait_ge(x2_stored, 16 * (B + 1))
            y_ready(0)
            with pool.Fori(0, N_COMB // 2) as h:
                for s in range(2):
                    gather(0, 2 * h + s, s, h)
            y_ready(1)
            for c in range(N_COMB, NQ):
                gather(1, c, c % 2, c // 2)

        @block.scalar
        def _(act):
            for name in ("h_c", "h_x", "h_a", "h_z", "expk", "v_copied", "expq", "gate", "egap"):
                act.sem_inc(SEMS[name], PER[name])
            act.sem_inc(MOE["h_m"], 2)
            for n in range(5):
                for k in range(KT):
                    act.wait_ge(w_turned, n * KT + k + 1)
                    nc.scalar.copy(w_hi(n)[:, k, :], tp[(n * KT + k) % 2][:, :, :].rearrange("p a c -> p (a c)")).then_inc(w_high, 1)

            def high(kind, b, i, src=None):
                if kind == "c":
                    act.wait_ge(SEMS["v"], nth("v", b, i - 2))
                if kind == "a":
                    act.wait_ge(SEMS["wo"], nth("wo", b, i - 2))
                dst = x2T[:, i, :, :] if kind == "z" else halves(kind, i)[0]
                act.wait_ge(SEMS["t_" + kind], nth("t_" + kind, b, i))
                src = src if src is not None else tp_bank("h_z" if kind == "z" else "l_" + kind, i)[:, :, :]
                nc.scalar.copy(dst, src).then_inc(SEMS["h_" + kind], 1)

            LAST = B - 1

            def exp_gap(b, t):
                act.wait_ge(SEMS["gap"], nth("gap", b, t))
                nc.scalar.activation(egap[:, :], gap[:, :], ACT.Exp).then_inc(SEMS["egap"], 1)

            def keys(b, before_):
                for step, kind, i in KEYS:
                    if step == "T" and kind == "z":
                        if before_ is not None:
                            high("z", before_, i)
                    elif step == "T":
                        high(kind, b, i)
                    elif step == "P":
                        act.wait_ge(SEMS["k"], nth("k", b, i))
                        act.wait_ge(SEMS["khat"], nth("khat", b, i - 2)) if i >= 2 else act.wait_ge(SEMS["qhat"], nth("qhat", b, i - 2))
                        nc.scalar.activation(expk[:, i % 2, :], pj_bank("khat", i)[:, :], ACT.Exp).then_inc(SEMS["expk"], 1)
                        act.wait_ge(SEMS["v"], nth("v", b, i))
                        act.wait_ge(SEMS["kv"], nth("kv", b, i - 2))
                        nc.scalar.copy(vones[:, i % 2, :, 0:P], pj_bank("v_copied", i)[:, :].rearrange("p (g c) -> p g c", g=G)).then_inc(SEMS["v_copied"], 1)
                        if before_ is None and i == 0:
                            act.wait_ge(e0_loaded, 16)
                            nc.scalar.copy(R[:, 0, :, :], wraw[:, 1, :, :]).then_inc(e0_high, 1)
                    elif step == "L" and before_ is not None:
                        exp_gap(before_, i)

            def queries(b):
                for step, kind, i in QUERIES:
                    if step == "T":
                        high(kind, b, i)
                    elif step == "Q":
                        act.wait_ge(SEMS["q"], nth("q", b, i))
                        act.wait_ge(SEMS["qhat"], nth("qhat", b, i - 2)) if i >= 2 else act.wait_ge(SEMS["khat"], nth("khat", b, ST + i - 2))
                        nc.scalar.activation(expq[:, i % 2, :], pj_bank("qhat", i)[:, :], ACT.Exp).then_inc(SEMS["expq"], 1)
                    elif step == "G":
                        if i == 0:
                            act.wait_ge(x2_stored, b * 16 + 16)
                            act.wait_ge(SEMS["x2n"], nth("x2n", b, -1))
                        act.wait_ge(SEMS["g"], nth("g", b, i))
                        nc.scalar.activation(gate[:, i, :], pj_bank("gate", i)[:, :], ACT.Sigmoid).then_inc(SEMS["gate"], 1)

            keys(0, None)
            with act.Fori(0, B - 1) as b:
                queries(b)
                keys(b + 1, b)
            queries(B - 1)

            def high_m(m, slot):
                act.wait_ge(MOE["t_m"], mth(m))
                act.wait_ge(MOE["m_done"], mth(m - 2))
                nc.scalar.copy(xsT_hi[:, slot, :, :], tp[slot][:, :, :]).then_inc(MOE["h_m"], 1)

            def store_y(g, m, slot):
                act.wait_ge(MOE["y_copied"], mth(m))
                act.dma_start(y_dram[g][bass.ds((m - FIRST[g]) * P, P), :], y_sb[slot]).then_inc(y_stored[slot], 16)

            def store_out(c, slot):
                act.wait_ge(combined, c + 1)
                act.dma_start(out_rows[bass.ds(c * P, P), :], x2r[:, slot, :]).then_inc(out_stored[slot], 16)

            for step, kind, i in START:
                if step == "T" and kind == "m":
                    high_m(i, i % 2)
                elif step == "T":
                    high("z", LAST, i, late_z[i % 2])
                elif step == "M":
                    store_y(0, i, i % 2)
                elif step == "L":
                    exp_gap(LAST, i)
            with act.Fori(0, (FIRST[1] - LOOP1) // 2) as h:
                for s in range(2):
                    high_m(2 * h + LOOP1 + s + 1, (LOOP1 + s + 1) % 2)
                    store_y(0, 2 * h + LOOP1 + s, (LOOP1 + s) % 2)
            for m in range(FIRST[1], LOOP2):
                high_m(m + 1, (m + 1) % 2)
                store_y(1, m, m % 2)
            with act.Fori(0, N_COMB // 2 - 1) as h:
                for s in range(2):
                    high_m(2 * h + LOOP2 + s + 1, (LOOP2 + s + 1) % 2)
                    store_y(1, 2 * h + LOOP2 + s, (LOOP2 + s) % 2)
                    store_out(2 * h + s, s)
            for s in range(2):
                m = M_ALL - 2 + s
                if m + 1 < M_ALL:
                    high_m(m + 1, (m + 1) % 2)
                store_y(1, m, m % 2)
                store_out(N_COMB - 2 + s, s)
            for c in range(N_COMB, NQ):
                store_out(c, c % 2)
            for s in range(2):
                act.wait_ge(out_stored[s], 16 + 16 * NQ // 2)

        @block.vector
        def _(dve):
            for name in ("l_c", "l_x", "l_a", "khat", "kvbd", "qhat", "mean", "num", "x2", "mean2", "logit_copied",
                         "gap", "picked", "ranked", "slot"):
                dve.sem_inc(SEMS[name], PER[name])
            for name in ("l_m", "y_copied"):
                dve.sem_inc(MOE[name], 2)
            n_step = [0, 0, 0]

            def link(ins):
                n_step[0] += 1
                ins.then_inc(dve_step, 1)
                dve.wait_ge(dve_step, n_step[2] * n_step[1] + n_step[0])

            def passed():
                dve.sem_inc(dve_passed, 1)

            for n in range(5):
                for k in range(KT):
                    dve.wait_ge(w_high, n * KT + k + 1)
                    nc.vector.tensor_tensor(w_lo(n)[:, k, :], tp[(n * KT + k) % 2][:, :, :].rearrange("p a c -> p (a c)"),
                                            w_hi(n)[:, k, :].bitcast(F32), ALU.subtract).then_inc(w_low, 1)
                if n == 1:
                    dve.wait_ge(small_loaded, 48)
                    link(nc.vector.tensor_copy(bias, bias_raw))
                    nc.vector.tensor_tensor(bias[32:64, :], bias_raw[32:64, :], bias[32:64, :].bitcast(F32), ALU.subtract).then_inc(bias_cut, 1)

            LAST = B - 1

            def low(kind, b, i):
                hi, lo = halves(kind, i)
                dve.wait_ge(SEMS["h_" + kind], nth("h_" + kind, b, i))
                nc.vector.tensor_tensor(lo, tp_bank("l_" + kind, i)[:, :, :], hi.bitcast(F32), ALU.subtract).then_inc(SEMS["l_" + kind], 1)

            def stats_x(b, t):
                if t == 0:
                    dve.wait_ge(x_loaded, b * 16 + 16)
                link(nc.vector.bn_stats(stats[:, :], x_raw[:, t, :]))
                passed()
                agg = nc.vector.bn_aggr(mv[:, 0, t, :], stats[:, :])
                if t < TT - 1:
                    link(agg)
                else:
                    agg.then_inc(SEMS["mean"], 1)
                    dve.wait_ge(SEMS["mean"], nth("mean", b, 0))

            def pick_two(b, t, bank):
                q = bass.ds(b * TT + t, 1)
                dve.wait_ge(SEMS["logit"], nth("logit", b, t))
                nc.vector.tensor_copy(lg[:, :], bank[:, 0:E]).then_inc(SEMS["logit_copied"], 1)
                dve.wait_ge(SEMS["logit_copied"], nth("logit_copied", b, t))
                passed()
                link(nc.vector.max(top[:, :], lg[:, :]))
                nc.vector.tensor_tensor(gap[:, :], top[:, 1:2], top[:, 0:1], ALU.subtract).then_inc(SEMS["gap"], 1)
                link(nc.vector.max_index(idx8[:, :], top[:, :], lg[:, :]))
                link(nc.vector.tensor_copy(idf[:, t, :], idx8[:, :]))
                link(nc.vector.tensor_tensor(both[:, :, :], iota8[:, :].rearrange("p (a e) -> p a e", a=1).broadcast_to((P, 2, E)),
                                             idf[:, t, 0:2].rearrange("p (a e) -> p a e", e=1).broadcast_to((P, 2, E)), ALU.is_equal))
                nc.vector.tensor_scalar(onehot[:, q, :, :].rearrange("p a j e -> p (a j) e"), both[:, :, :], 1.0, None, ALU.mult)
                nc.vector.tensor_tensor(members[:, t % 2, :], both[:, 0, :], both[:, 1, :], ALU.add).then_inc(SEMS["picked"], 1)
                dve.wait_ge(SEMS["egap"], nth("egap", b, t))
                link(nc.vector.tensor_scalar(total[:, :], egap[:, :], 1.0, None, ALU.add))
                link(nc.vector.reciprocal(w_top[:, 0:1], total[:, :]))
                link(nc.vector.tensor_tensor(w_top[:, 1:2], egap[:, :], w_top[:, 0:1], ALU.mult))
                link(nc.vector.tensor_scalar(wts[:, q, :].rearrange("p a j -> p (a j)"), w_top[:, :], 1.0, None, ALU.mult))

            def rank_two(g, b, t, bank):
                q = bass.ds(b * TT + t, 1)
                dve.wait_ge(SEMS["prefix"], nth("prefix", b, t))
                link(nc.vector.tensor_tensor(pos[:, :], bank[:, 0:E], run[:, g, :], ALU.add))
                nc.vector.tensor_tensor(run[:, g, :], bank[:, E:2 * E], run[:, g, :], ALU.add).then_inc(SEMS["ranked"], 1)
                dve.wait_ge(SEMS["ranked"], nth("ranked", b, t))
                link(nc.vector.tensor_tensor(prod[:, :, :], onehot[:, q, :, :].rearrange("p a j e -> p (a j) e"),
                                             pos[:, :].rearrange("p (a e) -> p a e", a=1).broadcast_to((P, 2, E)), ALU.mult))
                link(nc.vector.tensor_reduce(rank_t[:, :], prod[:, :, :], AX_X, ALU.add))
                link(nc.vector.tensor_scalar(rank[:, q, :].rearrange("p a j -> p (a j)"), rank_t[:, :], 1.0, None, ALU.mult))
                nc.vector.scalar_tensor_tensor(xidx[:, t, :], idf[:, t, 0:2], float(ROWS[g]), rank_t[:, :], ALU.mult, ALU.add).then_inc(SEMS["slot"], 1)
                dve.wait_ge(SEMS["slot"], nth("slot", b, t))

            def keys(b, before_):
                for step, kind, i in KEYS:
                    if step == "T" and kind != "z":
                        low(kind, b, i)
                    elif step == "P":
                        dve.wait_ge(SEMS["mink"], nth("mink", b, i))
                        dve.wait_ge(SEMS["kv"], nth("kv", b, i - 2))
                        nc.vector.scalar_tensor_tensor(khat[:, i % 2, :], pj_bank("khat", i)[:, :], 1.0, expk[:, i % 2, :],
                                                       ALU.add, ALU.max).then_inc(SEMS["khat"], 1)
                        if before_ is None and i == 1:
                            dve.wait_ge(e0_high, 1)
                            nc.vector.tensor_tensor(R[:, 1, :, :], wraw[:, 1, :, :], R[:, 0, :, :].bitcast(F32), ALU.subtract).then_inc(we_ready, 1)
                        if i in (2, 3):
                            stats_x(b, 2 * i - 4)
                            stats_x(b, 2 * i - 3)
                    elif step == "L" and before_ is not None:
                        pick_two(before_, i, pj_bank("logit_copied", i))
                    elif step == "K" and before_ is not None:
                        rank_two(0, before_, i, pj_bank("ranked", i))
                dve.wait_ge(SEMS["kv"], nth("kv", b, ST - 1))
                for h in range(2):
                    m = mask[:, :].rearrange("p (a c) -> p a c", a=1).broadcast_to((P, 2, CW))
                    last = nc.vector.tensor_tensor(kvbd[:, 2 * h:2 * h + 2, :], kvp[h], m, ALU.mult)
                last.then_inc(SEMS["kvbd"], 1)

            def attend(b, t):
                banks = [pj_bank("num", t, h) for h in range(2)]
                dve.wait_ge(SEMS["at"], nth("at", b, t))
                for h in range(2):
                    last = nc.vector.tensor_scalar(
                        den[:, t % 2, 8 * h:8 * h + 8].rearrange("p (g c) -> p g c", g=2),
                        banks[h][:, 0:2 * CW].rearrange("p (g c) -> p g c", g=2)[:, :, P:CW], ATTN_EPS, None, ALU.add)
                link(last)
                link(nc.vector.reciprocal(z[:, t % 2, :], den[:, t % 2, :]))
                dve.wait_ge(SEMS["t_a"], nth("t_a", b, t - 2)) if t >= 2 else dve.wait_ge(SEMS["t_x"], nth("t_x", b, TT - 1))
                for h in range(2):
                    for g in range(2):
                        zz = z[:, t % 2, 8 * h + 4 * g:8 * h + 4 * g + 4].rearrange("p (c a) -> p c a", a=1)
                        last = nc.vector.tensor_tensor(
                            num[:, t % 2, (2 * h + g) * P:(2 * h + g + 1) * P].rearrange("p (c e) -> p c e", c=HG),
                            banks[h][:, g * CW:g * CW + P].rearrange("p (c e) -> p c e", c=HG), zz.broadcast_to((P, HG, HD)), ALU.mult)
                last.then_inc(SEMS["num"], 1)

            def residual(b, t):
                dve.wait_ge(SEMS["wo"], nth("wo", b, t))
                nc.vector.tensor_tensor(x2[:, t, :], pj_bank("x2", t)[:, :], x_raw[:, t, :], ALU.add).then_inc(SEMS["x2"], 1)
                dve.wait_ge(SEMS["x2"], nth("x2", b, t))
                link(nc.vector.bn_stats(stats[:, :], x2[:, t, :]))
                passed()
                nc.vector.bn_aggr(mv[:, 1, t, :], stats[:, :]).then_inc(SEMS["mean2"], 1)
                dve.wait_ge(SEMS["mean2"], nth("mean2", b, t))

            def queries(b):
                for step, kind, i in QUERIES:
                    if step == "T":
                        low(kind, b, i)
                    elif step == "Q":
                        dve.wait_ge(SEMS["minq"], nth("minq", b, i))
                        nc.vector.scalar_tensor_tensor(qhat[:, i, :], pj_bank("qhat", i)[:, :], 1.0, expq[:, i % 2, :],
                                                       ALU.add, ALU.max).then_inc(SEMS["qhat"], 1)
                    elif step == "A":
                        attend(b, i)
                    elif step == "O":
                        residual(b, i)

            def plan(g, tmp):
                T, N, q0 = TILES[g], GROUP_TILES[g], g * GROUP_TILES[0]
                big = tmp[:, 0:T * E].rearrange("p (t e) -> p t e", t=T)

                def over(ap, n):
                    return ap.rearrange("p (a e) -> p a e", a=1).broadcast_to((P, n, E))

                def each(ap, n):
                    return ap.rearrange("p (a e) -> p a e", e=1).broadcast_to((P, ap.shape[1], n))

                nc.vector.scalar_tensor_tensor(pad_row[:, g, :], iota8[:, :], float(ROWS[g]), run[:, g, :], ALU.mult, ALU.add)
                cmp_ = tmp[:, 0:E * N].rearrange("p (e t) -> p e t", e=E)
                link(nc.vector.tensor_tensor(cmp_, each(run[:, g, :], N),
                                             steps[:, 0:N].rearrange("p (a t) -> p a t", a=1).broadcast_to((P, E, N)), ALU.is_gt))
                link(nc.vector.tensor_reduce(nt[:, 1:1 + E], cmp_, AX_X, ALU.add))
                sq = tmp[:, 0:E * E].rearrange("p (e f) -> p e f", e=E)
                link(nc.vector.tensor_tensor(sq, below[:, :, :], over(nt[:, 1:1 + E], E), ALU.mult))
                link(nc.vector.tensor_reduce(tb[:, :], sq, AX_X, ALU.add))
                link(nc.vector.tensor_tensor(last_t[:, :], tb[:, E - 1:E], nt[:, E:E + 1], ALU.add))
                link(nc.vector.tensor_scalar(last_t[:, :], last_t[:, :], 1.0, None, ALU.subtract))
                link(nc.vector.tensor_scalar(tile_t[:, 0:T], iota_t[:, 0:T], last_t[:, 0:1], None, ALU.min))
                link(nc.vector.tensor_tensor(big, each(tile_t[:, 0:T], E), over(tb[:, :], T), ALU.is_ge))
                link(nc.vector.tensor_reduce(tile_e[:, 0:T], big, AX_X, ALU.add))
                link(nc.vector.tensor_scalar(tile_e[:, 0:T], tile_e[:, 0:T], 1.0, None, ALU.subtract))
                link(nc.vector.tensor_tensor(big, big, over(nt[:, 0:E], T), ALU.mult))
                link(nc.vector.tensor_reduce(tile_b[:, 0:T], big, AX_X, ALU.add))
                link(nc.vector.tensor_tensor(tile_t[:, 0:T], tile_t[:, 0:T], tile_b[:, 0:T], ALU.subtract))
                nc.vector.tensor_copy(tile_expert[:, FIRST[g]:FIRST[g] + T], tile_e[:, 0:T])
                link(nc.vector.tensor_scalar(tile_b[:, 0:T], tile_e[:, 0:T], float(ROWS[g]), None, ALU.mult))
                link(nc.vector.scalar_tensor_tensor(tile_row[:, FIRST[g]:FIRST[g] + T], tile_t[:, 0:T], float(P), tile_b[:, 0:T], ALU.mult, ALU.add))
                tok = tmp[:, 0:2 * N * E].rearrange("p (q e) -> p q e", e=E)
                ys = yslot[:, q0:q0 + N, :].rearrange("p q j -> p (q j)")
                link(nc.vector.tensor_tensor(tok, onehot[:, q0:q0 + N, :, :].rearrange("p q j e -> p (q j) e"), over(tb[:, :], 2 * N), ALU.mult))
                link(nc.vector.tensor_reduce(ys, tok, AX_X, ALU.add))
                nc.vector.scalar_tensor_tensor(ys, ys, float(P), rank[:, q0:q0 + N, :].rearrange("p q j -> p (q j)"), ALU.mult, ALU.add).then_inc(planned, 1)
                dve.wait_ge(planned, g + 1)

            dve.wait_ge(consts, 9)
            keys(0, None)
            start, per = n_step[0], 2 * TT - 1 + TT + 8 * TT + 4 * TT + 2 * TT
            with dve.Fori(0, B - 1) as b:
                n_step[1:] = [per, b]
                queries(b)
                keys(b + 1, b)
                assert n_step[0] == start + per, (n_step, start, per)
            n_step[:] = [start + per * (B - 1), 0, 0]
            plan(0, vones.rearrange("p s g c -> p (s g c)"))
            queries(B - 1)

            def low_m(m, slot):
                dve.wait_ge(MOE["h_m"], mth(m))
                nc.vector.tensor_tensor(xsT_lo[:, slot, :, :], tp[slot][:, :, :], xsT_hi[:, slot, :, :].bitcast(F32), ALU.subtract).then_inc(MOE["l_m"], 1)

            def copy_y(m, slot, n):
                e = dve.value_load(tile_expert[0:1, bass.ds(m, 1)], min_val=0, max_val=E - 1)
                dve.wait_ge(MOE["m_done"], mth(m))
                dve.wait_ge(y_stored[slot], 16 * n + 16)
                nc.vector.tensor_tensor(y_sb[slot], pj[slot][:, :], be_all[:, bass.ds(e, 1), :].rearrange("p a d -> p (a d)"), ALU.add).then_inc(MOE["y_copied"], 1)

            def index(c, slot, n):
                dve.wait_ge(combined, c - 1) if not isinstance(c, int) or c >= 2 else None
                nc.vector.tensor_scalar(gidx[:, slot, :], yslot[:, bass.ds(c, 1), :].rearrange("p a j -> p (a j)"), 1.0, None, ALU.mult).then_inc(gidx_done, 1)

            def combine(c, slot, n):
                w = [wts[:, bass.ds(c, 1), j:j + 1].rearrange("p a j -> p (a j)") for j in range(2)]
                dve.wait_ge(gathered[slot], 32 * n + 32)
                dve.wait_ge(x2r_loaded[slot], 16 * n + 16)
                link_c(nc.vector.scalar_tensor_tensor(x2r[:, slot, :], yg[:, 2 * slot, :], w[0], x2r[:, slot, :], ALU.mult, ALU.add), c)
                nc.vector.scalar_tensor_tensor(x2r[:, slot, :], yg[:, 2 * slot + 1, :], w[1], x2r[:, slot, :], ALU.mult, ALU.add).then_inc(combined, 1)

            def link_c(ins, c):
                ins.then_inc(half_combined, 1)
                dve.wait_ge(half_combined, c + 1)

            dve.wait_ge(be_loaded, 16 * E)
            for step, kind, i in START:
                if step == "T" and kind == "m":
                    low_m(i, i % 2)
                elif step == "M":
                    copy_y(i, i % 2, i // 2)
                elif step == "L":
                    pick_two(LAST, i, pj[2 + i % 2])
                elif step == "K":
                    rank_two(1, LAST, i, pj[2 + i % 2])
            plan(1, qhat[:, 2:4, :].rearrange("p s d -> p (s d)"))
            with dve.Fori(0, (FIRST[1] - LOOP1) // 2) as h:
                for s in range(2):
                    low_m(2 * h + LOOP1 + s + 1, (LOOP1 + s + 1) % 2)
                    copy_y(2 * h + LOOP1 + s, (LOOP1 + s) % 2, h + (LOOP1 + s) // 2)
            for m in range(FIRST[1], LOOP2):
                low_m(m + 1, (m + 1) % 2)
                copy_y(m, m % 2, m // 2)
            index(0, 0, 0)
            index(1, 1, 0)
            with dve.Fori(0, N_COMB // 2 - 1) as h:
                for s in range(2):
                    low_m(2 * h + LOOP2 + s + 1, (LOOP2 + s + 1) % 2)
                    copy_y(2 * h + LOOP2 + s, (LOOP2 + s) % 2, h + (LOOP2 + s) // 2)
                    combine(2 * h + s, s, h)
                    index(2 * h + s + 2, s, h + 1)
            for s in range(2):
                m, c = M_ALL - 2 + s, N_COMB - 2 + s
                if m + 1 < M_ALL:
                    low_m(m + 1, (m + 1) % 2)
                copy_y(m, m % 2, m // 2)
                combine(c, s, c // 2)
                index(c + 2, s, 0)
            for c in range(N_COMB, NQ):
                combine(c, c % 2, c // 2)
                if c + 2 < NQ:
                    index(c + 2, c % 2, 0)

        @block.tensor
        def _(pe):
            for name in ("t_c", "t_x", "t_a", "t_z", "k", "v", "kv", "q", "g", "at", "wo", "logit", "prefix"):
                pe.sem_inc(SEMS[name], PER[name])
            for name in ("t_m", "m_done"):
                pe.sem_inc(MOE[name], 2)
            pe.wait_ge(pool_step, 2)
            for n in range(5):
                pe.wait_ge(w_loaded[n % 2], 16 * (n // 2 + 1))
                for k in range(KT):
                    u = n * KT + k
                    if u >= 2:
                        pe.wait_ge(w_low, u - 1)
                    for a in range(4):
                        last = nc.tensor.transpose(tp[u % 2][:, a, :], wraw[:, n % 2, a, k * P:(k + 1) * P], ident[:, :])
                    last.then_inc(w_turned, 1)
            pe.wait_ge(w_low, 5 * KT)
            pe.wait_ge(bias_cut, 1)
            pe.wait_ge(consts, 9)
            LAST = B - 1

            def free(uses, banks, b, name, i, second=0):
                n = uses.index((name, i)) + second
                was, j = uses[n - len(banks)]
                bb = b if n >= len(banks) else b - 1
                if was in OF_BATCH_BEFORE:
                    bb = bb - 1
                pe.wait_ge(SEMS[was], nth(was, bb, j))
                return banks[n % len(banks)]

            def turn(kind, b, i, src, bank=None):
                if bank is None:
                    bank = free(TP_USES, tp, b, "l_" + kind, i) if kind != "z" else free(TP_USES, tp, b + 1, "h_z", i)
                for k in range(KT):
                    last = nc.tensor.transpose(bank[:, k, :], src[:, k * P:(k + 1) * P], ident[:, :])
                last.then_inc(SEMS["t_" + kind], 1)

            def three(bank, s_hi, s_lo, m_hi, m_lo, with_bias=False):
                for k in range(KT):
                    nc.tensor.matmul(bank[:, :], s_hi(k), m_hi(k), start=(k == 0), stop=False)
                    nc.tensor.matmul(bank[:, :], s_hi(k), m_lo(k), start=False, stop=False)
                    last = nc.tensor.matmul(bank[:, :], s_lo(k), m_hi(k), start=False, stop=(k == KT - 1 and not with_bias))
                if with_bias:
                    last = nc.tensor.matmul(bank[:, :], pick, bias, start=False, stop=True)
                return last

            def logits_of(b, t, bank):
                pe.wait_ge(SEMS["h_z"], nth("h_z", b, t))
                for k in range(KT):
                    last = nc.tensor.matmul(bank[:, 0:E], x2T[:, t, k, :], wr_sb[:, k, :], start=(k == 0), stop=(k == KT - 1))
                last.then_inc(SEMS["logit"], 1)

            def prefix_of(b, t, bank):
                pe.wait_ge(SEMS["picked"], nth("picked", b, t))
                nc.tensor.matmul(bank[:, 0:E], before[:, :], members[:, t % 2, :], start=True, stop=True, skip_group_check=True)
                nc.tensor.matmul(bank[:, E:2 * E], ones[:, :], members[:, t % 2, :], start=True, stop=True,
                                 skip_group_check=True).then_inc(SEMS["prefix"], 1)

            def keys(b, before_):
                for step, kind, i in KEYS:
                    if step == "T" and kind == "c":
                        pe.wait_ge(ctx_loaded[(i // 2) % 2], b * 32 + 16 * (i // 4 + 1))
                        turn("c", b, i, ctx_raw[:, (i // 2) % 2, i % 2, :])
                    elif step == "T" and kind == "x":
                        pe.wait_ge(SEMS["xn"], nth("xn", b, i))
                        turn("x", b, i, xn[:, i % 2, :])
                    elif step == "T" and before_ is not None:
                        pe.wait_ge(SEMS["x2n"], nth("x2n", before_, i))
                        turn("z", before_, i, x2n[:, i % 2, :])
                    elif step == "P":
                        pe.wait_ge(SEMS["l_c"], nth("l_c", b, i))
                        for w, done, used in ((WK, "k", "khat"), (WV, "v", "v_copied")):
                            bank = free(PJ_USES, pj, b, used, i)
                            three(bank, lambda k: ctxT_hi[:, i % 2, k, :], lambda k: ctxT_lo[:, i % 2, k, :],
                                  lambda k: w_hi(w)[:, k, :], lambda k: w_lo(w)[:, k, :]).then_inc(SEMS[done], 1)
                    elif step == "L" and before_ is not None:
                        logits_of(before_, i, free(PJ_USES, pj, b, "logit_copied", i))
                    elif step == "K" and before_ is not None:
                        prefix_of(before_, i, free(PJ_USES, pj, b, "ranked", i))
                    elif step == "KV":
                        pe.wait_ge(SEMS["khat"], nth("khat", b, i))
                        pe.wait_ge(SEMS["v_copied"], nth("v_copied", b, i))
                        if i == 0:
                            pe.wait_ge(SEMS["kvbd"], nth("kvbd", b, -1))
                        for g in range(G):
                            last = nc.tensor.matmul(kvp[g // 2][:, g % 2, :], khat[:, i % 2, g * P:(g + 1) * P], vones[:, i % 2, g, :],
                                                    start=(i == 0 and g % 2 == 0), stop=(i == ST - 1), skip_group_check=True)
                        last.then_inc(SEMS["kv"], 1)

            def queries(b):
                for step, kind, i in QUERIES:
                    if step == "Q":
                        if i == 0:
                            pe.wait_ge(SEMS["l_x"], nth("l_x", b, TT - 1))
                        three(free(PJ_USES, pj, b, "qhat", i), lambda k: w_hi(WQ)[:, k, i * P:(i + 1) * P], lambda k: w_lo(WQ)[:, k, i * P:(i + 1) * P],
                              lambda k: xT_hi[:, k, :], lambda k: xT_lo[:, k, :]).then_inc(SEMS["q"], 1)
                    elif step == "G":
                        three(free(PJ_USES, pj, b, "gate", i), lambda k: xT_hi[:, k, i * P:(i + 1) * P], lambda k: xT_lo[:, k, i * P:(i + 1) * P],
                              lambda k: w_hi(WG)[:, k, :], lambda k: w_lo(WG)[:, k, :], with_bias=True).then_inc(SEMS["g"], 1)
                    elif step == "A":
                        if i == 0:
                            pe.wait_ge(SEMS["kvbd"], nth("kvbd", b, 0))
                            pe.wait_ge(SEMS["qhat"], nth("qhat", b, G - 1))
                        for h in range(2):
                            bank = free(PJ_USES, pj, b, "num", i, h)
                            for g in range(2 * h, 2 * h + 2):
                                last = nc.tensor.matmul(bank[:, (g % 2) * CW:(g % 2 + 1) * CW], qhat[:, g, i * P:(i + 1) * P], kvbd[:, g, :],
                                                        start=True, stop=True, skip_group_check=True)
                        last.then_inc(SEMS["at"], 1)
                    elif step == "T":
                        pe.wait_ge(SEMS["ag"], nth("ag", b, i))
                        turn("a", b, i, num[:, i % 2, :])
                    elif step == "O":
                        pe.wait_ge(SEMS["l_a"], nth("l_a", b, i))
                        three(free(PJ_USES, pj, b, "x2", i), lambda k: agT_hi[:, i % 2, k, :], lambda k: agT_lo[:, i % 2, k, :],
                              lambda k: w_hi(WO)[:, k, :], lambda k: w_lo(WO)[:, k, :]).then_inc(SEMS["wo"], 1)

            keys(0, None)
            with pe.Fori(0, B - 1) as b:
                queries(b)
                keys(b + 1, b)
            queries(B - 1)

            def turn_m(m, slot, n):
                pe.wait_ge(xs_loaded[slot], 16 * n + 16)
                pe.wait_ge(MOE["l_m"], mth(m - 2))
                for k in range(KT):
                    last = nc.tensor.transpose(tp[slot][:, k, :], xs_raw[:, slot, k * P:(k + 1) * P], ident[:, :])
                last.then_inc(MOE["t_m"], 1)

            def expert(m, slot):
                e = pe.value_load(tile_expert[0:1, bass.ds(m, 1)], min_val=0, max_val=E - 1)
                pe.wait_ge(we_ready, e + 1)
                pe.wait_ge(MOE["l_m"], mth(m))
                pe.wait_ge(MOE["y_copied"], mth(m - 2))

                def part(block_of, k):
                    return R[:, bass.ds(block_of, 1), k, :].rearrange("p a d -> p (a d)")

                three(pj[slot], lambda k: xsT_hi[:, slot, k, :], lambda k: xsT_lo[:, slot, k, :],
                      lambda k: part(2 * e, k), lambda k: part(2 * e + 1, k)).then_inc(MOE["m_done"], 1)

            pe.wait_ge(SEMS["x2"], nth("x2", LAST, TT - 1))
            pe.wait_ge(SEMS["l_a"], nth("l_a", LAST, TT - 1))
            for step, kind, i in START:
                if step == "T" and kind == "m":
                    turn_m(i, i % 2, i // 2)
                elif step == "M":
                    expert(i, i % 2)
                elif step == "T":
                    pe.wait_ge(SEMS["x2n"], nth("x2n", LAST, i))
                    pe.wait_ge(SEMS["h_z"], nth("h_z", LAST, i - 2))
                    turn("z", LAST, i, x2n[:, i, :] if i < 2 else num[:, i - 2, :], late_z[i % 2])
                elif step == "L":
                    pe.wait_ge(SEMS["ranked"], nth("ranked", LAST, i - 2))
                    logits_of(LAST, i, pj[2 + i % 2])
                elif step == "K":
                    pe.wait_ge(SEMS["logit_copied"], nth("logit_copied", LAST, i))
                    prefix_of(LAST, i, pj[2 + i % 2])
            with pe.Fori(0, (FIRST[1] - LOOP1) // 2) as h:
                for s in range(2):
                    turn_m(2 * h + LOOP1 + s + 1, (LOOP1 + s + 1) % 2, h + (LOOP1 + s + 1) // 2)
                    expert(2 * h + LOOP1 + s, (LOOP1 + s) % 2)
            for m in range(FIRST[1], LOOP2):
                turn_m(m + 1, (m + 1) % 2, (m + 1) // 2)
                expert(m, m % 2)
            with pe.Fori(0, N_COMB // 2 - 1) as h:
                for s in range(2):
                    turn_m(2 * h + LOOP2 + s + 1, (LOOP2 + s + 1) % 2, h + (LOOP2 + s + 1) // 2)
                    expert(2 * h + LOOP2 + s, (LOOP2 + s) % 2)
            for m in range(M_ALL - 2, M_ALL):
                if m + 1 < M_ALL:
                    turn_m(m + 1, (m + 1) % 2, (m + 1) // 2)
                expert(m, m % 2)


_INS = ["x", "ctx_2048", "L0_xattn_Wq", "L0_xattn_Wg", "L0_xattn_bg", "L0_xattn_Wkv", "L0_xattn_Wo",
        "L0_ffn_Wr", "L0_ffn_We", "L0_ffn_be"]
_OUTS = [((4, 512, 512), "float32")]


def kernel(**inputs):
    import numpy as _np
    import concourse.bacc as _bacc
    from concourse import mybir as _mybir
    from concourse.bass_utils import run_bass_kernel_spmd as _run

    nc = _bacc.Bacc("TRN2", target_bir_lowering=False, num_devices=1)
    arrays, args = {}, []
    for name in _INS:
        a = _np.ascontiguousarray(inputs[name])
        arrays[f"in_{name}_dram"] = a
        args.append(nc.dram_tensor(f"in_{name}_dram", a.shape, _mybir.dt.from_np(a.dtype), kind="ExternalInput").ap())
    for i, (shape, dtype) in enumerate(_OUTS):
        dt = _mybir.dt.from_np(_np.dtype(dtype))
        args.append(nc.dram_tensor(f"out_{i}_dram", shape, dt, kind="ExternalOutput").ap())
    xattn_moe_kernel(nc, *args)
    r = _run(nc, [arrays], core_ids=[0])
    got = tuple(r.results[0][f"out_{i}_dram"] for i in range(len(_OUTS)))
    return got[0]
```

```python
from contextlib import ExitStack

import concourse.bass as bass
from concourse import mybir

F32 = mybir.dt.float32
F32R = mybir.dt.float32r
BF16 = mybir.dt.bfloat16
U32 = mybir.dt.uint32
I32 = mybir.dt.int32
ALU = mybir.AluOpType
ACT = mybir.ActivationFunctionType
AX_X = mybir.AxisListType.X

P = 128
HEADS = 16
ATTN_EPS = 1e-6
NORM_EPS = 1e-5


def xattn_moe_kernel(nc, x, ctx_in, wq_t, wg_t, bg, wkv_t, wo_t, wr, we, be, out):
    B, L, D = x.shape
    S = ctx_in.shape[1]
    E = we.shape[0]
    KT = D // P
    ST = S // P
    TT = L // P
    G = D // P
    HG = HEADS // G
    HD = D // HEADS
    CW = P + HG
    assert L == D == 512 and ST == 8 and TT == KT == 4 and E == 8

    GROUP_TILES = ((B - 1) * TT, TT)
    ROWS = [n * P + P for n in GROUP_TILES]
    TILES = [2 * n + E - 1 for n in GROUP_TILES]
    FIRST = [0, TILES[0]]
    M_ALL = sum(TILES)
    NQ = B * TT

    xs_dram = [nc.dram_tensor(f"xs{g}", [E * ROWS[g], D], F32, kind="Internal").ap() for g in range(2)]
    y_dram = [nc.dram_tensor(f"y{g}", [TILES[g] * P, D], F32, kind="Internal").ap() for g in range(2)]
    x2_dram = nc.dram_tensor("x2_rows", [B * L, D], F32, kind="Internal").ap()
    out_rows = out.rearrange("b l d -> (b l) d")

    with ExitStack() as stack:
        def sb(name, shape, dt=F32):
            return stack.enter_context(nc.sbuf_tensor(name, shape, dt))

        def sem(name):
            return stack.enter_context(nc.semaphore(name))

        R = sb("R", [P, 2 * E, KT, D], F32R)
        WK, WV, WQ, WG, WO = range(5)

        def w_hi(n):
            return R[:, 2 + 2 * n, :, :]

        def w_lo(n):
            return R[:, 3 + 2 * n, :, :]

        xT_hi, xT_lo = R[:, 12, :, :], R[:, 13, :, :]
        ctxT_hi = R[:, 14, 0:2, :].rearrange("p s (k c) -> p s k c", k=KT)
        ctxT_lo = R[:, 14, 2:4, :].rearrange("p s (k c) -> p s k c", k=KT)
        agT_hi = R[:, 15, 0:2, :].rearrange("p s (k c) -> p s k c", k=KT)
        agT_lo = R[:, 15, 2:4, :].rearrange("p s (k c) -> p s k c", k=KT)
        aux = sb("aux", [P, 4, D], F32R)
        xsT_hi = aux[:, 0:2, :].rearrange("p s (k c) -> p s k c", k=KT)
        xsT_lo = aux[:, 2:4, :].rearrange("p s (k c) -> p s k c", k=KT)

        wraw = sb("wraw", [P, 2, KT, D])
        w_raw = [wraw[:, 0, :, :], wraw[:, 1, :, :]]
        x_raw = wraw[:, 1, :, :]
        e_raw = wraw[:, 0, :, :]
        BUF = 4 * D + G * 2 * CW + 2 * D
        buf = sb("buf", [P, BUF])
        ctx_raw = buf[:, 0:4 * D].rearrange("p (s t d) -> p s t d", s=2, t=2)
        vones = buf[:, 4 * D:4 * D + 2 * G * CW].rearrange("p (s g c) -> p s g c", s=2, g=G)
        expk = buf[:, 4 * D + 2 * G * CW:BUF].rearrange("p (s d) -> p s d", s=2)
        expq = expk
        be_all = buf[:, 0:E * D].rearrange("p (e d) -> p e d", e=E)
        khat = sb("khat", [P, 2, D])
        xs_raw = khat
        kvbd = sb("kvbd", [P, G, CW])
        zeros = sb("zeros", [P, D])
        bias = sb("bias", [P, D])
        y_sb = [kvbd[:, :, :].rearrange("p g c -> p (g c)")[:, 0:D], zeros[:, :]]
        num = sb("num", [P, 2, D])
        qhat = sb("qhat", [P, G, L])
        x2T = qhat[:, :, :].rearrange("p t (k c) -> p t k c", k=KT)
        gate = sb("gate", [P, TT, D])
        x2 = gate
        w_raw += [gate[:, :, :], qhat[:, :, :], w_raw[0]]
        normed = sb("normed", [P, 2, D])
        xn = [normed[:, 0, :], normed[:, 1, :], num[:, 0, :], num[:, 1, :]]
        yg = [(qhat[:, 0, :], qhat[:, 1, :]), (qhat[:, 2, :], qhat[:, 3, :]), (xn[0], xn[1]), (xn[2], xn[3])]
        x2r = wraw[:, :, :, :].rearrange("p s t d -> p (s t) d")

        ident = sb("ident", [P, P])
        before = sb("before", [P, P], BF16)
        ones = sb("ones", [P, P], BF16)
        full = [num[:, 0, 0:P], num[:, 0, P:2 * P]]
        mask = sb("mask", [P, CW])
        wr_sb = sb("wr_sb", [P, KT, E])
        iota8 = sb("iota8", [P, E])
        iota_t = sb("iota_t", [P, max(TILES)])
        steps = sb("steps", [P, max(GROUP_TILES)])
        below = sb("below", [P, E, E])
        stats = sb("stats", [P, 6])
        mv = sb("mv", [P, 2, TT, 2])
        rstd = sb("rstd", [P, 2, TT])
        mhalf = sb("mhalf", [P, TT])
        shift = sb("shift", [P, 2, TT])
        den = sb("den", [P, 2, HEADS])
        z = sb("z", [P, 2, HEADS])
        lg = sb("lg", [P, E])
        top = sb("top", [P, E])
        gap = sb("gap", [P, 1])
        egap = sb("egap", [P, 1])
        total = sb("total", [P, 1])
        idx8 = sb("idx8", [P, E], U32)
        idf = sb("idf", [P, TT, E])
        both = sb("both", [P, 2, E])
        members = sb("members", [P, 2, E], BF16)
        w_top = sb("w_top", [P, 2])
        pos = sb("pos", [P, E])
        prod = sb("prod", [P, 2, E])
        rank_t = sb("rank_t", [P, 2])
        run = sb("run", [P, 2, E])
        onehot = sb("onehot", [P, NQ, 2, E])
        rank = sb("rank", [P, NQ, 2])
        wts = sb("wts", [P, NQ, 2])
        yslot = sb("yslot", [P, NQ, 2])
        xidx = sb("xidx", [P, TT, 2], U32)
        gidx = sb("gidx", [P, 4, 2], U32)
        nt = sb("nt", [P, 1 + E])
        tb = sb("tb", [P, E])
        last_t = sb("last_t", [P, 1])
        tile_t = sb("tile_t", [P, max(TILES)])
        tile_e = sb("tile_e", [P, max(TILES)])
        tile_b = sb("tile_b", [P, max(TILES)])
        tile_expert = sb("tile_expert", [P, M_ALL], I32)
        tile_row = sb("tile_row", [P, M_ALL], I32)
        pad_row = sb("pad_row", [P, 2, E], I32)

        tp = [stack.enter_context(nc.psum_tensor(f"tp{i}", [P, KT, P], F32)) for i in range(2)]
        pj = [stack.enter_context(nc.psum_tensor(f"pj{i}", [P, D], F32)) for i in range(4)]
        kvb = [stack.enter_context(nc.psum_tensor(f"kvb{i}", [P, D], F32)) for i in range(2)]
        late_z = [a[:, :].rearrange("p (k c) -> p k c", k=KT) for a in kvb]
        kvp = [a[:, 0:2 * CW].rearrange("p (g c) -> p g c", g=2) for a in kvb]

        w_loaded = [sem(f"w_loaded{i}") for i in range(2 * 4 + 3)]
        ctx_first = sem("ctx_first")
        small_loaded, x_loaded, be_loaded = sem("small_loaded"), sem("x_loaded"), sem("be_loaded")
        ctx_loaded = [sem(f"ctx_loaded{i}") for i in range(2)]
        x2_stored = sem("x2_stored")
        scattered = [sem(f"scattered{i}") for i in range(TT)]
        padded = [sem(f"padded{g}") for g in range(2)]
        xs_loaded = [sem(f"xs_loaded{i}") for i in range(2)]
        y_stored = [sem(f"y_stored{i}") for i in range(2)]
        gathered = [sem(f"gathered{i}") for i in range(4)]
        x2r_loaded = [sem(f"x2r_loaded{i}") for i in range(2)]
        x2r_late = [sem(f"x2r_late{i}") for i in range(4)]
        out_stored = [sem(f"out_stored{i}") for i in range(4)]
        e_loaded = [sem(f"e_loaded{i}") for i in range(2)]
        consts, zeroed = sem("consts"), sem("zeroed")
        w_high, w_low = sem("w_high"), sem("w_low")
        e_high, we_ready = sem("e_high"), sem("we_ready")
        planned = sem("planned")
        half_combined = sem("half_combined")
        gidx_done, combined = sem("gidx_done"), sem("combined")
        dve_step, pool_step = sem("dve_step"), sem("pool_step")
        dve_passed, pool_passed = sem("dve_passed"), sem("pool_passed")

        PER = {
            "t_c": ST, "h_c": ST, "l_c": ST, "t_x": TT, "h_x": TT, "l_x": TT, "t_a": TT, "h_a": TT, "l_a": TT,
            "t_z": TT, "h_z": TT, "k": ST, "v": ST, "kv": ST, "q": G, "g": TT, "at": TT, "wo": TT,
            "logit": TT, "prefix": TT, "expk": ST, "khat": ST, "v_copied": ST, "kvbd": 1,
            "expq": G, "qhat": G, "biased": TT, "gate": TT, "mean_x": 1, "scale_x": 1, "xn": TT, "ag": TT,
            "x2": TT, "mean_x2": TT, "scale_x2": TT, "x2n": TT, "logit_copied": TT, "gap": TT, "egap": TT, "picked": TT,
            "ranked": TT, "slot": TT,
        }
        SEMS = {name: sem(name) for name in PER}

        def nth(name, b, i):
            return (b + 1) * PER[name] + i + 1

        MOE = {name: sem(name) for name in ("t_m", "h_m", "l_m", "m_done", "y_copied")}

        def mth(m):
            return m + 3

        KEYS = []
        turn_before = {1: ("z", 0), 2: ("z", 1), 3: ("z", 2), 4: ("z", 3), 6: ("x", 0), 7: ("x", 1)}
        logits = {1: 0, 2: 1, 3: 2, 4: 3}
        prefixes = {2: 0, 3: 1, 4: 2, 5: 3}
        for i in range(ST):
            KEYS += [("T", *turn_before[i])] if i in turn_before else []
            KEYS += [("P", "k", i), ("T", "c", i + 1) if i + 1 < ST else ("T", "x", 2), ("P", "v", i)]
            KEYS += [("L", "", logits[i])] if i in logits else []
            KEYS += [("K", "", prefixes[i])] if i in prefixes else []
            KEYS += [("T", "x", 3)] if i == ST - 1 else []
            KEYS += [("KV", "", i - 1)] if i >= 1 else []
        KEYS += [("KV", "", ST - 1)]
        QUERIES = [("Q", "", g) for g in range(G)]
        QUERIES += [("G", "", 0), ("A", "", 0), ("G", "", 1), ("A", "", 1), ("T", "a", 0), ("G", "", 2), ("A", "", 2),
                    ("T", "a", 1), ("O", "", 0), ("G", "", 3), ("A", "", 3), ("T", "a", 2), ("O", "", 1), ("T", "a", 3),
                    ("O", "", 2), ("T", "c", 0), ("O", "", 3)]

        TP_USES, PJ_USES = [], []
        for step, kind, i in KEYS + QUERIES:
            if step == "T":
                TP_USES.append(("h_z", i, -1) if kind == "z" else ("l_" + kind, i, 0))
            else:
                PJ_USES += {"P": [("expk" if kind == "k" else "v_copied", i, 0)], "L": [("logit_copied", i, -1)],
                            "K": [("ranked", i, -1)], "KV": [], "Q": [("expq", i, 0)], "G": [("biased", i, 0)],
                            "A": [("ag", i, 0)] * 2, "O": [("x2", i, 0)]}[step]
        TP_USES = TP_USES[-1:] + TP_USES[:-1]
        assert TP_USES[0] == ("l_c", 0, 0) and len(TP_USES) % 2 == 0 and len(PJ_USES) % 4 == 0

        def place(uses, name, i, second=0):
            return [use[:2] for use in uses].index((name, i)) + second

        def tp_bank(name, i):
            return tp[place(TP_USES, name, i) % 2]

        def halves(kind, i):
            if kind == "x":
                return xT_hi[:, :, i * P:(i + 1) * P], xT_lo[:, :, i * P:(i + 1) * P]
            hi, lo = (ctxT_hi, ctxT_lo) if kind == "c" else (agT_hi, agT_lo)
            return hi[:, i % 2, :, :], lo[:, i % 2, :, :]

        def pj_bank(name, i, second=0):
            return pj[place(PJ_USES, name, i, second) % 4]

        CHUNKS = {}
        for step, kind, i in KEYS:
            if step in ("L", "K") or kind == "z":
                CHUNKS[step, i] = 2 * KT + len(CHUNKS)
        assert len(CHUNKS) == 3 * KT

        def chunk_loaded(u):
            return w_loaded[u if u < 2 * KT else 2 * KT + u // KT - 2]

        def tiles(m):
            return [("T", "m", m + 1), ("M", "", m)]

        START = tiles(0) + [("T", "z", 0), ("T", "z", 1)] + tiles(1) + [("L", "", 0), ("T", "z", 2)] + tiles(2)
        START += [("L", "", 1), ("T", "z", 3)] + tiles(3) + [("K", "", 0)] + tiles(4) + [("L", "", 2)] + tiles(5)
        START += [("K", "", 1)] + tiles(6) + [("L", "", 3)] + tiles(7) + [("K", "", 2)] + tiles(8) + [("K", "", 3)]
        START += tiles(9) + tiles(10) + tiles(11) + tiles(12)
        LOOP1 = 13
        N_COMB = GROUP_TILES[0]
        LOOP2 = M_ALL - N_COMB
        assert (FIRST[1] - LOOP1) % 2 == 0 and N_COMB == 12 and LOOP2 % 2 == 0 and LOOP2 > FIRST[1]

        def res_tile(c):
            return x2r[:, bass.ds(c, 1), :].rearrange("p a d -> p (a d)")

        block = stack.enter_context(nc.Block())

        @block.sync
        def _(sp):
            srcs = [wkv_t[:, 0:D], wkv_t[:, D:2 * D], wq_t, wg_t, wo_t]

            def load_w_chunks(n):
                for k in range(KT):
                    sp.dma_start(w_raw[n][:, k, :], srcs[n][k * P:(k + 1) * P, :]).then_inc(chunk_loaded(KT * n + k), 16)

            def load_w(n):
                sp.dma_start(w_raw[n], srcs[n].rearrange("(k p) d -> p k d", p=P)).then_inc(chunk_loaded(KT * n), 16)

            def ctx_pair(b, j):
                sp.wait_ge(SEMS["t_c"], nth("t_c", b, 2 * j - 3))
                sp.dma_start(ctx_raw[:, j % 2, :, :],
                             ctx_in[b, 2 * j * P:(2 * j + 2) * P, :].rearrange("(t p) d -> p t d", p=P)).then_inc(ctx_loaded[j % 2], 16)

            def store_x2(b):
                sp.wait_ge(SEMS["x2"], nth("x2", b, TT - 1))
                sp.dma_start(x2_dram[bass.ds(b * L, L), :].rearrange("(t p) d -> p t d", p=P), x2[:, :, :]).then_inc(x2_stored, 16)

            def load_x(b):
                sp.dma_start(x_raw, x[b, :, :].rearrange("(t p) d -> p t d", p=P)).then_inc(x_loaded, 16)

            sp.dma_start(ctx_raw[:, 0, 0, :], ctx_in[0, 0:P, :]).then_inc(ctx_first, 16)
            load_w_chunks(WK)
            sp.dma_start(ctx_raw[:, 0, 1, :], ctx_in[0, P:2 * P, :]).then_inc(ctx_loaded[0], 16)
            load_w_chunks(WV)
            sp.dma_start(wr_sb[:, :, :], wr.rearrange("(k p) e -> p k e", p=P)).then_inc(small_loaded, 16)
            sp.dma_start(bias[:, :], bg.rearrange("(a d) -> a d", a=1).broadcast_to((P, D))).then_inc(small_loaded, 16)
            load_w(WQ)
            ctx_pair(0, 1)
            load_w(WG)
            sp.wait_ge(w_low, KT)
            load_w(WO)
            sp.wait_ge(w_low, 2 * KT)
            load_x(0)
            ctx_pair(0, 2)
            ctx_pair(0, 3)
            with sp.Fori(0, B - 1) as b:
                ctx_pair(b + 1, 0)
                ctx_pair(b + 1, 1)
                store_x2(b)
                load_x(b + 1)
                ctx_pair(b + 1, 2)
                ctx_pair(b + 1, 3)

            def load_tile(g, m, slot):
                row = sp.value_load(tile_row[0:1, bass.ds(m, 1)], min_val=0, max_val=E * ROWS[g] - P)
                sp.wait_ge(MOE["t_m"], mth(m - 2))
                sp.dma_start(xs_raw[:, slot, :], xs_dram[g][bass.ds(row, P), :]).then_inc(xs_loaded[slot], 16)

            def pad(g, e, src):
                row = sp.value_load(pad_row[0:1, g, bass.ds(e, 1)], min_val=0, max_val=E * ROWS[g] - P)
                sp.dma_start(xs_dram[g][bass.ds(row, P), :], src).then_inc(padded[g], 16)

            def load_x2r(c, n, loaded):
                sp.dma_start(x2r[:, c % 8:c % 8 + n, :], x2_dram[c * P:(c + n) * P, :].rearrange("(t p) d -> p t d", p=P)).then_inc(loaded, 16)

            PAIRS = (FIRST[1] - 3) // 2
            sp.wait_ge(planned, 1)
            sp.wait_ge(zeroed, 1)
            with sp.Fori(0, E) as e:
                pad(0, e, zeros[:, :])
            sp.wait_ge(padded[0], 16 * E)
            for t in range(TT):
                sp.wait_ge(scattered[t], 32 * (B - 1))
            load_tile(0, 0, 0)
            load_tile(0, 1, 1)
            sp.wait_ge(SEMS["qhat"], nth("qhat", B - 1, G - 1))
            for e in range(E):
                sp.dma_start(be_all[:, e, :], be[e:e + 1, :].broadcast_to((P, D))).then_inc(be_loaded, 16)
            load_tile(0, 2, 0)
            sp.wait_ge(x2_stored, 16 * B)
            sp.wait_ge(SEMS["x2"], nth("x2", B - 1, TT - 1))
            load_x2r(4, 4, x2r_loaded[1])
            with sp.Fori(0, PAIRS - 4) as h:
                load_tile(0, 2 * h + 3, 1)
                load_tile(0, 2 * h + 4, 0)
            sp.wait_ge(planned, 2)
            sp.wait_ge(zeroed, 2)
            for m in range(FIRST[1] - E, FIRST[1]):
                load_tile(0, m, m % 2)
                e = m - (FIRST[1] - E)
                pad(1, e, bias[:, :])
                if e == 4:
                    sp.wait_ge(we_ready, 2 * E)
                if e >= 4:
                    load_x2r(e - 4, 1, x2r_loaded[0])
            sp.wait_ge(padded[1], 16 * E)
            for t in range(TT):
                sp.wait_ge(scattered[t], 32 * B)
            for m in range(FIRST[1], LOOP2):
                load_tile(1, m, m % 2)
            with sp.Fori(0, 3) as h:
                for s in range(2):
                    load_tile(1, 2 * h + LOOP2 + s, s)
            for m in range(LOOP2 + 6, M_ALL):
                load_tile(1, m, m % 2)
                c = m - LOOP2 + 2
                if c < N_COMB:
                    sp.wait_ge(out_stored[c % 4], 16)
                    load_x2r(c, 1, x2r_late[c % 4])

        @block.gpsimd
        def _(pool):
            for s in range(2):
                pool.sem_inc(y_stored[s], 16)
            for name in ("scale_x", "scale_x2"):
                pool.sem_inc(SEMS[name], PER[name])
            pool.sem_inc(x2_stored, 16)
            pool.sem_inc(combined, 4)
            n_step = [0, 0, 0]

            def link(ins):
                n_step[0] += 1
                ins.then_inc(pool_step, 1)
                pool.wait_ge(pool_step, n_step[2] * n_step[1] + n_step[0])

            def passed():
                pool.sem_inc(pool_passed, 1)

            nc.gpsimd.memset(zeros[:, :], 0.0).then_inc(zeroed, 1)
            link(nc.gpsimd.memset(ident[:, :], 0.0))
            link(nc.gpsimd.affine_select(out=ident[:, :], in_=ident[:, :], compare_op=ALU.not_equal, fill=1.0,
                                         base=0, pattern=[[-1, P]], channel_multiplier=1))
            link(nc.gpsimd.memset(full[1], 1.0))
            nc.gpsimd.memset(vones[:, :, :, P:CW], 1.0).then_inc(consts, 1)
            nc.gpsimd.memset(mhalf[:, :], -0.5).then_inc(consts, 1)
            nc.gpsimd.memset(nt[:, 0:1], 0.0).then_inc(consts, 1)
            nc.gpsimd.memset(run[:, :, :], 0.0).then_inc(consts, 1)
            nc.gpsimd.iota(iota8[:, :], pattern=[[1, E]], base=0, channel_multiplier=0,
                           allow_small_or_imprecise_dtypes=True).then_inc(consts, 1)
            nc.gpsimd.iota(iota_t[:, :], pattern=[[1, max(TILES)]], base=0, channel_multiplier=0,
                           allow_small_or_imprecise_dtypes=True).then_inc(consts, 1)
            nc.gpsimd.iota(steps[:, :], pattern=[[P, max(GROUP_TILES)]], base=0, channel_multiplier=0,
                           allow_small_or_imprecise_dtypes=True).then_inc(consts, 1)
            link(nc.gpsimd.memset(mask[:, :], 1.0))
            m4 = mask[:, 0:P].rearrange("p (h e) -> p h e", h=HG)
            for ap, pat in ((m4, [[-HD, HG], [0, HD]]), (mask[:, P:CW], [[-HD, HG]])):
                link(nc.gpsimd.affine_select(out=ap, in_=ap, compare_op=ALU.is_ge, fill=0.0, base=0,
                                             pattern=pat, channel_multiplier=1))
                link(nc.gpsimd.affine_select(out=ap, in_=ap, compare_op=ALU.is_ge, fill=0.0, base=HD - 1,
                                             pattern=[[-s, c] for s, c in pat], channel_multiplier=-1))
            link(nc.gpsimd.memset(full[0], 0.0))
            link(nc.gpsimd.affine_select(out=full[0], in_=full[0], compare_op=ALU.is_ge, fill=1.0,
                                         base=0, pattern=[[-1, P]], channel_multiplier=1))
            link(nc.gpsimd.memset(below[:, :, :], 0.0))
            link(nc.gpsimd.affine_select(out=below[:, :, :], in_=below[:, :, :], compare_op=ALU.is_ge, fill=1.0,
                                         base=0, pattern=[[-1, E], [1, E]], channel_multiplier=0))
            nc.gpsimd.tensor_copy(before[:, :], full[0]).then_inc(consts, 1)
            nc.gpsimd.tensor_copy(ones[:, :], full[1]).then_inc(consts, 1)

            def scatter(g, b, t):
                pool.wait_ge(SEMS["slot"], nth("slot", b, t))
                passed()
                for j in range(2):
                    nc.gpsimd.indirect_dma_start(out=xs_dram[g][:, :], out_offset=bass.IndirectOffsetOnAxis(ap=xidx[:, t, j:j + 1], axis=0),
                                                 in_=xn[t], in_offset=None).then_inc(scattered[t], 16)

            def scale(k, t0, n, name, b, i):
                pool.wait_ge(SEMS["mean" + name], nth("mean" + name, b, i))
                passed()
                link(nc.gpsimd.tensor_tensor(rstd[:, k, t0:t0 + n], rstd[:, k, t0:t0 + n], mhalf[:, 0:n], ALU.pow))
                nc.gpsimd.tensor_tensor(shift[:, k, t0:t0 + n], shift[:, k, t0:t0 + n], rstd[:, k, t0:t0 + n],
                                        ALU.mult).then_inc(SEMS["scale" + name], 1)

            def load_expert(e, h):
                pool.dma_start(e_raw[:, 2 * h:2 * h + 2, :],
                               we[e, h * 2 * P:(h + 1) * 2 * P, :].rearrange("(k p) f -> p k f", p=P)).then_inc(e_loaded[h], 16)

            def cut_expert(e, h):
                ks = slice(2 * h, 2 * h + 2)
                pool.wait_ge(e_loaded[h], 16 * (e + 1))
                nc.gpsimd.tensor_copy(R[:, 2 * e, ks, :], e_raw[:, ks, :]).then_inc(e_high, 1)
                pool.wait_ge(e_high, 2 * e + h + 1)
                nc.gpsimd.tensor_tensor(R[:, 2 * e + 1, ks, :], e_raw[:, ks, :], R[:, 2 * e, ks, :].bitcast(F32),
                                        ALU.subtract).then_inc(we_ready, 1)
                if e + 1 < E:
                    pool.wait_ge(we_ready, 2 * e + h + 1)
                    load_expert(e + 1, h)

            scale(0, 0, TT, "_x", 0, 0)
            pool.wait_ge(w_low, 5 * KT)
            load_expert(0, 0)
            load_expert(0, 1)
            cut_expert(0, 0)
            cut_expert(0, 1)
            start, per = n_step[0], TT + 1
            with pool.Fori(0, B - 1) as b:
                n_step[1:] = [per, b]
                for t in range(TT):
                    scale(1, t, 1, "_x2", b, t)
                scatter(0, b, 0)
                scatter(0, b, 1)
                scale(0, 0, TT, "_x", b + 1, 0)
                scatter(0, b, 2)
                scatter(0, b, 3)
                assert n_step[0] == start + per
            n_step[:] = [start + per * (B - 1), 0, 0]
            last = B - 1
            pool.wait_ge(SEMS["v"], nth("v", last, ST - 1))
            for h in range(4):
                cut_expert(1 + h // 2, h % 2)
            for t in range(TT):
                scale(1, t, 1, "_x2", last, t)
            pool.wait_ge(SEMS["wo"], nth("wo", last, TT - 1))
            nc.gpsimd.memset(bias[:, :], 0.0).then_inc(zeroed, 1)
            for e in range(3, E):
                for h in range(2):
                    cut_expert(e, h)
            for t in range(TT):
                scatter(1, last, t)

            def gather(g, c, slot):
                pool.wait_ge(gidx_done, c + 1)
                pool.wait_ge(combined, c + 1)
                passed()
                for j in range(2):
                    nc.gpsimd.indirect_dma_start(out=yg[slot][j], out_offset=None, in_=y_dram[g][:, :],
                                                 in_offset=bass.IndirectOffsetOnAxis(ap=gidx[:, slot, j:j + 1], axis=0)).then_inc(gathered[slot], 16)

            def y_ready(g):
                n = FIRST[g] + TILES[g]
                pool.wait_ge(y_stored[0], 16 + 16 * ((n + 1) // 2))
                pool.wait_ge(y_stored[1], 16 + 16 * (n // 2))

            for t in range(TT):
                pool.wait_ge(scattered[t], 32 * B)
            y_ready(0)
            with pool.Fori(0, N_COMB // 4) as h:
                for s in range(4):
                    gather(0, 4 * h + s, s)
            y_ready(1)
            for c in range(N_COMB, NQ):
                gather(1, c, c % 4)

        @block.scalar
        def _(act):
            for name in ("h_c", "h_x", "h_a", "h_z", "expk", "v_copied", "expq", "gate", "xn", "x2n", "egap"):
                act.sem_inc(SEMS[name], PER[name])
            act.sem_inc(MOE["h_m"], 2)

            def high_w(u):
                act.wait_ge(chunk_loaded(u), 16)
                nc.scalar.copy(w_hi(u // KT)[:, u % KT, :], w_raw[u // KT][:, u % KT, :]).then_inc(w_high, 1)

            def high(kind, b, i, src=None):
                if kind == "c":
                    act.wait_ge(SEMS["v"], nth("v", b, i - 2))
                if kind == "a":
                    act.wait_ge(SEMS["wo"], nth("wo", b, i - 2))
                dst = x2T[:, i, :, :] if kind == "z" else halves(kind, i)[0]
                act.wait_ge(SEMS["t_" + kind], nth("t_" + kind, b, i))
                src = src if src is not None else tp_bank("h_z" if kind == "z" else "l_" + kind, i)[:, :, :]
                nc.scalar.copy(dst, src).then_inc(SEMS["h_" + kind], 1)

            LAST = B - 1

            def exp_gap(b, t):
                act.wait_ge(SEMS["gap"], nth("gap", b, t))
                nc.scalar.activation(egap[:, :], gap[:, :], ACT.Exp).then_inc(SEMS["egap"], 1)

            def norm(k, t, name, b, src):
                nc.scalar.activation(xn[t], src, ACT.Identity, bias=shift[:, k, t:t + 1], scale=rstd[:, k, t:t + 1]).then_inc(SEMS[name], 1)

            def norm_x(b, t, before_):
                act.wait_ge(SEMS["scale_x"], nth("scale_x", b, 0))
                if before_ is not None:
                    act.wait_ge(scattered[t], 32 * before_ + 32)
                    act.wait_ge(SEMS["t_z"], nth("t_z", before_, t))
                norm(0, t, "xn", b, x_raw[:, t, :])

            def norm_x2(b, t):
                act.wait_ge(SEMS["scale_x2"], nth("scale_x2", b, t))
                if t >= 2:
                    act.wait_ge(SEMS["t_a"], nth("t_a", b, t))
                norm(1, t, "x2n", b, x2[:, t, :])

            def keys(b, before_):
                for step, kind, i in KEYS:
                    if before_ is None and (step, i) in CHUNKS and kind in ("", "z"):
                        high_w(CHUNKS[step, i])
                    elif step == "T":
                        high(kind, b if kind != "z" else before_, i)
                    elif step == "P" and kind == "k":
                        act.wait_ge(SEMS["k"], nth("k", b, i))
                        act.wait_ge(SEMS["kv"], nth("kv", b, i - 2))
                        nc.scalar.activation(khat[:, i % 2, :], pj_bank("expk", i)[:, :], ACT.Relu)
                        act.wait_ge(SEMS["khat"], nth("khat", b, i - 2)) if i >= 2 else act.wait_ge(SEMS["qhat"], nth("qhat", b, i - 2))
                        nc.scalar.activation(expk[:, i % 2, :], pj_bank("expk", i)[:, :], ACT.Exp).then_inc(SEMS["expk"], 1)
                    elif step == "P":
                        act.wait_ge(SEMS["v"], nth("v", b, i))
                        act.wait_ge(SEMS["kv"], nth("kv", b, i - 2))
                        nc.scalar.copy(vones[:, i % 2, :, 0:P], pj_bank("v_copied", i)[:, :].rearrange("p (g c) -> p g c", g=G)).then_inc(SEMS["v_copied"], 1)
                        if i == 0 and before_ is not None:
                            norm_x2(before_, TT - 1)
                        if i in (4, 5):
                            norm_x(b, i - 4, before_)
                        if i == 6:
                            norm_x(b, 2, before_)
                            norm_x(b, 3, before_)
                    elif step == "L":
                        exp_gap(before_, i)

            def queries(b):
                for step, kind, i in QUERIES:
                    if step == "T" and kind == "c":
                        if b is LAST:
                            high_m(0, 0)
                        else:
                            high("c", b + 1, 0)
                    elif step == "T":
                        high(kind, b, i)
                    elif step == "Q":
                        act.wait_ge(SEMS["q"], nth("q", b, i))
                        nc.scalar.activation(qhat[:, i, :], pj_bank("expq", i)[:, :], ACT.Relu)
                        act.wait_ge(SEMS["qhat"], nth("qhat", b, i - 2)) if i >= 2 else act.wait_ge(SEMS["khat"], nth("khat", b, ST + i - 2))
                        nc.scalar.activation(expq[:, i % 2, :], pj_bank("expq", i)[:, :], ACT.Exp).then_inc(SEMS["expq"], 1)
                    elif step == "G":
                        act.wait_ge(SEMS["biased"], nth("biased", b, i))
                        nc.scalar.activation(gate[:, i, :], gate[:, i, :], ACT.Sigmoid).then_inc(SEMS["gate"], 1)
                    elif step == "O" and i >= 1:
                        norm_x2(b, i - 1)

            def high_m(m, slot):
                act.wait_ge(MOE["t_m"], mth(m))
                act.wait_ge(MOE["m_done"], mth(m - 2))
                nc.scalar.copy(xsT_hi[:, slot, :, :], tp[slot][:, :, :]).then_inc(MOE["h_m"], 1)

            act.wait_ge(zeroed, 1)
            nc.scalar.activation(egap[:, :], zeros[:, 0:1], ACT.Exp)
            high_w(0)
            high("c", 0, 0)
            for u in range(1, 2 * KT):
                high_w(u)
            keys(0, None)
            with act.Fori(0, B - 1) as b:
                queries(b)
                keys(b + 1, b)
            queries(B - 1)

            def store_y(g, m, slot):
                act.wait_ge(MOE["y_copied"], mth(m))
                act.dma_start(y_dram[g][bass.ds((m - FIRST[g]) * P, P), :], y_sb[slot]).then_inc(y_stored[slot], 16)

            def store_out(c, slot, res):
                act.wait_ge(combined, c + 5)
                act.dma_start(out_rows[bass.ds(c * P, P), :], res).then_inc(out_stored[slot], 16)

            for step, kind, i in START:
                if step == "T" and kind == "m":
                    high_m(i, i % 2)
                elif step == "T":
                    high("z", LAST, i, late_z[i % 2])
                    if i == 0:
                        norm_x2(LAST, TT - 1)
                elif step == "M":
                    if i >= 1:
                        store_y(0, i - 1, (i - 1) % 2)
                elif step == "L":
                    exp_gap(LAST, i)
            with act.Fori(0, (FIRST[1] - LOOP1) // 2) as h:
                for s in range(2):
                    high_m(2 * h + LOOP1 + s + 1, (LOOP1 + s + 1) % 2)
                    store_y(0, 2 * h + LOOP1 + s - 1, (LOOP1 + s - 1) % 2)
            for m in range(FIRST[1], LOOP2 + 1):
                high_m(m + 1, (m + 1) % 2)
                store_y(0 if m == FIRST[1] else 1, m - 1, (m - 1) % 2)
            with act.Fori(0, N_COMB // 4 - 1) as h:
                for s in range(4):
                    high_m(4 * h + LOOP2 + s + 2, s % 2)
                    store_y(1, 4 * h + LOOP2 + s, s % 2)
                    store_out(4 * h + s, s, res_tile(4 * h + s))
            for s in range(4):
                m, c = M_ALL - 4 + s, N_COMB - 4 + s
                if m + 2 < M_ALL:
                    high_m(m + 2, m % 2)
                store_y(1, m, m % 2)
                store_out(c, s, x2r[:, c % 8, :])
            for c in range(N_COMB, NQ):
                store_out(c, c % 4, x2[:, c - N_COMB, :])
            for s in range(4):
                act.wait_ge(out_stored[s], 16 * NQ // 4)

        @block.vector
        def _(dve):
            for name in ("l_c", "l_x", "l_a", "khat", "kvbd", "qhat", "biased", "mean_x", "ag", "x2", "mean_x2",
                         "logit_copied", "ranked", "gap", "picked", "slot"):
                dve.sem_inc(SEMS[name], PER[name])
            for name in ("l_m", "y_copied"):
                dve.sem_inc(MOE[name], 2)
            n_step = [0, 0, 0]

            def link(ins):
                n_step[0] += 1
                ins.then_inc(dve_step, 1)
                dve.wait_ge(dve_step, n_step[2] * n_step[1] + n_step[0])

            def passed():
                dve.sem_inc(dve_passed, 1)

            def low_w(u):
                dve.wait_ge(w_high, u + 1)
                nc.vector.tensor_tensor(w_lo(u // KT)[:, u % KT, :], w_raw[u // KT][:, u % KT, :], w_hi(u // KT)[:, u % KT, :].bitcast(F32),
                                        ALU.subtract).then_inc(w_low, 1)

            LAST = B - 1

            def low(kind, b, i):
                hi, lo = halves(kind, i)
                dve.wait_ge(SEMS["h_" + kind], nth("h_" + kind, b, i))
                nc.vector.tensor_tensor(lo, tp_bank("l_" + kind, i)[:, :, :], hi.bitcast(F32), ALU.subtract).then_inc(SEMS["l_" + kind], 1)

            def low_m(m, slot):
                dve.wait_ge(MOE["h_m"], mth(m))
                nc.vector.tensor_tensor(xsT_lo[:, slot, :, :], tp[slot][:, :, :], xsT_hi[:, slot, :, :].bitcast(F32), ALU.subtract).then_inc(MOE["l_m"], 1)

            def stats_x(b, t):
                if t == 0:
                    dve.wait_ge(x_loaded, b * 16 + 16)
                link(nc.vector.bn_stats(stats[:, :], x_raw[:, t, :]))
                passed()
                agg = nc.vector.bn_aggr(mv[:, 0, t, :], stats[:, :])
                link(agg)
                if t == TT - 1:
                    centre(0, 0, TT, "mean_x")

            def centre(k, t0, n, name):
                nc.vector.tensor_scalar(shift[:, k, t0:t0 + n], mv[:, k, t0:t0 + n, 0], -1.0, None, ALU.mult)
                nc.vector.tensor_scalar(rstd[:, k, t0:t0 + n], mv[:, k, t0:t0 + n, 1], NORM_EPS, None, ALU.add).then_inc(SEMS[name], 1)

            def pick_two(b, t, bank):
                q = bass.ds(b * TT + t, 1)
                dve.wait_ge(SEMS["logit"], nth("logit", b, t))
                nc.vector.tensor_copy(lg[:, :], bank[:, 0:E]).then_inc(SEMS["logit_copied"], 1)
                dve.wait_ge(SEMS["logit_copied"], nth("logit_copied", b, t))
                passed()
                link(nc.vector.max(top[:, :], lg[:, :]))
                nc.vector.tensor_tensor(gap[:, :], top[:, 1:2], top[:, 0:1], ALU.subtract).then_inc(SEMS["gap"], 1)
                link(nc.vector.max_index(idx8[:, :], top[:, :], lg[:, :]))
                link(nc.vector.tensor_copy(idf[:, t, :], idx8[:, :]))
                link(nc.vector.tensor_tensor(both[:, :, :], iota8[:, :].rearrange("p (a e) -> p a e", a=1).broadcast_to((P, 2, E)),
                                             idf[:, t, 0:2].rearrange("p (a e) -> p a e", e=1).broadcast_to((P, 2, E)), ALU.is_equal))
                nc.vector.tensor_scalar(onehot[:, q, :, :].rearrange("p a j e -> p (a j) e"), both[:, :, :], 1.0, None, ALU.mult)
                nc.vector.tensor_tensor(members[:, t % 2, :], both[:, 0, :], both[:, 1, :], ALU.add).then_inc(SEMS["picked"], 1)
                dve.wait_ge(SEMS["egap"], nth("egap", b, t))
                link(nc.vector.tensor_scalar(total[:, :], egap[:, :], 1.0, None, ALU.add))
                link(nc.vector.reciprocal(w_top[:, 0:1], total[:, :]))
                link(nc.vector.tensor_tensor(w_top[:, 1:2], egap[:, :], w_top[:, 0:1], ALU.mult))
                link(nc.vector.tensor_scalar(wts[:, q, :].rearrange("p a j -> p (a j)"), w_top[:, :], 1.0, None, ALU.mult))

            def rank_two(g, b, t, bank):
                q = bass.ds(b * TT + t, 1)
                dve.wait_ge(SEMS["prefix"], nth("prefix", b, t))
                link(nc.vector.tensor_tensor(pos[:, :], bank[:, 0:E], run[:, g, :], ALU.add))
                nc.vector.tensor_tensor(run[:, g, :], bank[:, E:2 * E], run[:, g, :], ALU.add).then_inc(SEMS["ranked"], 1)
                dve.wait_ge(SEMS["ranked"], nth("ranked", b, t))
                link(nc.vector.tensor_tensor(prod[:, :, :], onehot[:, q, :, :].rearrange("p a j e -> p (a j) e"),
                                             pos[:, :].rearrange("p (a e) -> p a e", a=1).broadcast_to((P, 2, E)), ALU.mult))
                link(nc.vector.tensor_reduce(rank_t[:, :], prod[:, :, :], AX_X, ALU.add))
                link(nc.vector.tensor_scalar(rank[:, q, :].rearrange("p a j -> p (a j)"), rank_t[:, :], 1.0, None, ALU.mult))
                nc.vector.scalar_tensor_tensor(xidx[:, t, :], idf[:, t, 0:2], float(ROWS[g]), rank_t[:, :], ALU.mult, ALU.add).then_inc(SEMS["slot"], 1)
                dve.wait_ge(SEMS["slot"], nth("slot", b, t))

            def keys(b, before_):
                for step, kind, i in KEYS:
                    if before_ is None and (step, i) in CHUNKS and kind in ("", "z"):
                        low_w(CHUNKS[step, i])
                    elif step == "T" and kind != "z":
                        low(kind, b, i)
                    elif step == "P" and kind == "k":
                        dve.wait_ge(SEMS["expk"], nth("expk", b, i))
                        nc.vector.scalar_tensor_tensor(khat[:, i % 2, :], expk[:, i % 2, :], 1.0, khat[:, i % 2, :],
                                                       ALU.min, ALU.add).then_inc(SEMS["khat"], 1)
                    elif step == "P":
                        if i in (2, 3):
                            stats_x(b, 2 * i - 4)
                            stats_x(b, 2 * i - 3)
                    elif step == "L":
                        pick_two(before_, i, pj_bank("logit_copied", i))
                    elif step == "K":
                        rank_two(0, before_, i, pj_bank("ranked", i))
                dve.wait_ge(SEMS["kv"], nth("kv", b, ST - 1))
                for h in range(2):
                    m = mask[:, :].rearrange("p (a c) -> p a c", a=1).broadcast_to((P, 2, CW))
                    last = nc.vector.tensor_tensor(kvbd[:, 2 * h:2 * h + 2, :], kvp[h], m, ALU.mult)
                last.then_inc(SEMS["kvbd"], 1)

            def attend(b, t):
                banks = [pj_bank("ag", t, h) for h in range(2)]
                dve.wait_ge(SEMS["at"], nth("at", b, t))
                for h in range(2):
                    last = nc.vector.tensor_scalar(
                        den[:, t % 2, 8 * h:8 * h + 8].rearrange("p (g c) -> p g c", g=2),
                        banks[h][:, 0:2 * CW].rearrange("p (g c) -> p g c", g=2)[:, :, P:CW], ATTN_EPS, None, ALU.add)
                link(last)
                link(nc.vector.reciprocal(z[:, t % 2, :], den[:, t % 2, :]))
                dve.wait_ge(SEMS["t_a"], nth("t_a", b, t - 2)) if t >= 2 else dve.wait_ge(SEMS["t_x"], nth("t_x", b, TT - 1))
                for h in range(2):
                    for g in range(2):
                        zz = z[:, t % 2, 8 * h + 4 * g:8 * h + 4 * g + 4].rearrange("p (c a) -> p c a", a=1)
                        last = nc.vector.tensor_tensor(
                            num[:, t % 2, (2 * h + g) * P:(2 * h + g + 1) * P].rearrange("p (c e) -> p c e", c=HG),
                            banks[h][:, g * CW:g * CW + P].rearrange("p (c e) -> p c e", c=HG), zz.broadcast_to((P, HG, HD)), ALU.mult)
                link(last)
                dve.wait_ge(SEMS["gate"], nth("gate", b, t))
                nc.vector.tensor_tensor(num[:, t % 2, :], num[:, t % 2, :], gate[:, t, :], ALU.mult).then_inc(SEMS["ag"], 1)

            def residual(b, t):
                dve.wait_ge(SEMS["wo"], nth("wo", b, t))
                nc.vector.tensor_tensor(x2[:, t, :], pj_bank("x2", t)[:, :], x_raw[:, t, :], ALU.add).then_inc(SEMS["x2"], 1)
                dve.wait_ge(SEMS["x2"], nth("x2", b, t))
                link(nc.vector.bn_stats(stats[:, :], x2[:, t, :]))
                passed()
                link(nc.vector.bn_aggr(mv[:, 1, t, :], stats[:, :]))
                centre(1, t, 1, "mean_x2")

            def queries(b):
                for step, kind, i in QUERIES:
                    if step == "T" and kind == "c":
                        if b is LAST:
                            low_m(0, 0)
                        else:
                            low("c", b + 1, 0)
                    elif step == "T":
                        low(kind, b, i)
                    elif step == "Q":
                        dve.wait_ge(SEMS["expq"], nth("expq", b, i))
                        nc.vector.scalar_tensor_tensor(qhat[:, i, :], expq[:, i % 2, :], 1.0, qhat[:, i, :],
                                                       ALU.min, ALU.add).then_inc(SEMS["qhat"], 1)
                    elif step == "G":
                        if i == 0:
                            dve.wait_ge(x2_stored, b * 16 + 16)
                            dve.wait_ge(SEMS["x2n"], nth("x2n", b, -1))
                        dve.wait_ge(SEMS["g"], nth("g", b, i))
                        nc.vector.tensor_tensor(gate[:, i, :], pj_bank("biased", i)[:, :], bias[:, :], ALU.add).then_inc(SEMS["biased"], 1)
                    elif step == "A":
                        attend(b, i)
                    elif step == "O":
                        residual(b, i)

            def index(c, slot):
                nc.vector.tensor_scalar(gidx[:, slot, :], yslot[:, bass.ds(c, 1), :].rearrange("p a j -> p (a j)"), 1.0, None, ALU.mult).then_inc(gidx_done, 1)

            def plan(g, tmp):
                T, N, q0 = TILES[g], GROUP_TILES[g], g * GROUP_TILES[0]
                big = tmp[:, 0:T * E].rearrange("p (t e) -> p t e", t=T)

                def over(ap, n):
                    return ap.rearrange("p (a e) -> p a e", a=1).broadcast_to((P, n, E))

                def each(ap, n):
                    return ap.rearrange("p (a e) -> p a e", e=1).broadcast_to((P, ap.shape[1], n))

                nc.vector.scalar_tensor_tensor(pad_row[:, g, :], iota8[:, :], float(ROWS[g]), run[:, g, :], ALU.mult, ALU.add)
                cmp_ = tmp[:, 0:E * N].rearrange("p (e t) -> p e t", e=E)
                link(nc.vector.tensor_tensor(cmp_, each(run[:, g, :], N),
                                             steps[:, 0:N].rearrange("p (a t) -> p a t", a=1).broadcast_to((P, E, N)), ALU.is_gt))
                link(nc.vector.tensor_reduce(nt[:, 1:1 + E], cmp_, AX_X, ALU.add))
                sq = tmp[:, 0:E * E].rearrange("p (e f) -> p e f", e=E)
                link(nc.vector.tensor_tensor(sq, below[:, :, :], over(nt[:, 1:1 + E], E), ALU.mult))
                link(nc.vector.tensor_reduce(tb[:, :], sq, AX_X, ALU.add))
                link(nc.vector.tensor_tensor(last_t[:, :], tb[:, E - 1:E], nt[:, E:E + 1], ALU.add))
                link(nc.vector.tensor_scalar(last_t[:, :], last_t[:, :], 1.0, None, ALU.subtract))
                yield
                link(nc.vector.tensor_scalar(tile_t[:, 0:T], iota_t[:, 0:T], last_t[:, 0:1], None, ALU.min))
                link(nc.vector.tensor_tensor(big, each(tile_t[:, 0:T], E), over(tb[:, :], T), ALU.is_ge))
                link(nc.vector.tensor_reduce(tile_e[:, 0:T], big, AX_X, ALU.add))
                link(nc.vector.tensor_scalar(tile_e[:, 0:T], tile_e[:, 0:T], 1.0, None, ALU.subtract))
                link(nc.vector.tensor_tensor(big, big, over(nt[:, 0:E], T), ALU.mult))
                link(nc.vector.tensor_reduce(tile_b[:, 0:T], big, AX_X, ALU.add))
                link(nc.vector.tensor_tensor(tile_t[:, 0:T], tile_t[:, 0:T], tile_b[:, 0:T], ALU.subtract))
                nc.vector.tensor_copy(tile_expert[:, FIRST[g]:FIRST[g] + T], tile_e[:, 0:T])
                link(nc.vector.tensor_scalar(tile_b[:, 0:T], tile_e[:, 0:T], float(ROWS[g]), None, ALU.mult))
                link(nc.vector.scalar_tensor_tensor(tile_row[:, FIRST[g]:FIRST[g] + T], tile_t[:, 0:T], float(P), tile_b[:, 0:T], ALU.mult, ALU.add))
                yield
                tok = tmp[:, 0:2 * N * E].rearrange("p (q e) -> p q e", e=E)
                ys = yslot[:, q0:q0 + N, :].rearrange("p q j -> p (q j)")
                link(nc.vector.tensor_tensor(tok, onehot[:, q0:q0 + N, :, :].rearrange("p q j e -> p (q j) e"), over(tb[:, :], 2 * N), ALU.mult))
                link(nc.vector.tensor_reduce(ys, tok, AX_X, ALU.add))
                nc.vector.scalar_tensor_tensor(ys, ys, float(P), rank[:, q0:q0 + N, :].rearrange("p q j -> p (q j)"), ALU.mult, ALU.add).then_inc(planned, 1)
                dve.wait_ge(planned, g + 1)

            low_w(0)
            low("c", 0, 0)
            for u in range(1, 2 * KT):
                low_w(u)
            dve.wait_ge(small_loaded, 32)
            dve.wait_ge(consts, 9)
            keys(0, None)
            start, per = n_step[0], 2 * TT + 2 * TT + 8 * TT + 4 * TT + 3 * TT
            with dve.Fori(0, B - 1) as b:
                n_step[1:] = [per, b]
                queries(b)
                keys(b + 1, b)
                assert n_step[0] == start + per, (n_step, start, per)
            n_step[:] = [start + per * (B - 1), 0, 0]
            for _ in plan(0, vones.rearrange("p s g c -> p (s g c)")):
                pass
            for c in range(4):
                index(c, c)
            queries(B - 1)

            def copy_y(m, slot, n):
                e = dve.value_load(tile_expert[0:1, bass.ds(m, 1)], min_val=0, max_val=E - 1)
                dve.wait_ge(MOE["m_done"], mth(m))
                dve.wait_ge(y_stored[slot], 16 * n + 16)
                nc.vector.tensor_tensor(y_sb[slot], pj[slot][:, :], be_all[:, bass.ds(e, 1), :].rearrange("p a d -> p (a d)"), ALU.add).then_inc(MOE["y_copied"], 1)

            def combine(c, slot, n, res, following=True):
                w = [wts[:, bass.ds(c, 1), j:j + 1].rearrange("p a j -> p (a j)") for j in range(2)]
                dve.wait_ge(gathered[slot], 32 * n + 32)
                nc.vector.scalar_tensor_tensor(res, yg[slot][0], w[0], res, ALU.mult, ALU.add).then_inc(half_combined, 1)
                if following:
                    index(c + 4, slot)
                dve.wait_ge(half_combined, c + 1)
                nc.vector.scalar_tensor_tensor(res, yg[slot][1], w[1], res, ALU.mult, ALU.add).then_inc(combined, 1)

            dve.wait_ge(be_loaded, 16 * E)
            planning = plan(1, qhat[:, 2:4, :].rearrange("p s d -> p (s d)"))
            for step, kind, i in START:
                if step == "T" and kind == "m":
                    low_m(i, i % 2)
                elif step == "M":
                    copy_y(i, i % 2, i // 2)
                elif step == "L":
                    pick_two(LAST, i, pj[2 + i % 2])
                elif step == "K":
                    rank_two(1, LAST, i, pj[2 + i % 2])
                if step == "M" and i >= LOOP1 - 3:
                    next(planning, None)
            with dve.Fori(0, (FIRST[1] - LOOP1) // 2) as h:
                for s in range(2):
                    low_m(2 * h + LOOP1 + s + 1, (LOOP1 + s + 1) % 2)
                    copy_y(2 * h + LOOP1 + s, (LOOP1 + s) % 2, h + (LOOP1 + s) // 2)
            for m in range(FIRST[1], LOOP2):
                low_m(m + 1, (m + 1) % 2)
                copy_y(m, m % 2, m // 2)
            dve.wait_ge(x2r_loaded[0], 16 * 4)
            dve.wait_ge(x2r_loaded[1], 16)
            with dve.Fori(0, N_COMB // 4 - 1) as h:
                for s in range(4):
                    low_m(4 * h + LOOP2 + s + 1, (s + 1) % 2)
                    combine(4 * h + s, s, h, res_tile(4 * h + s))
                    copy_y(4 * h + LOOP2 + s, s % 2, 2 * h + (LOOP2 + s) // 2)
            for s in range(4):
                m, c = M_ALL - 4 + s, N_COMB - 4 + s
                if m + 1 < M_ALL:
                    low_m(m + 1, (m + 1) % 2)
                dve.wait_ge(x2r_late[s], 16)
                if m == M_ALL - 1:
                    copy_y(m, m % 2, m // 2)
                combine(c, s, c // 4, x2r[:, c % 8, :])
                if m < M_ALL - 1:
                    copy_y(m, m % 2, m // 2)
            for c in range(N_COMB, NQ):
                combine(c, c % 4, c // 4, x2[:, c - N_COMB, :], following=False)

        @block.tensor
        def _(pe):
            for name in ("t_c", "t_x", "t_a", "t_z", "k", "v", "kv", "q", "g", "at", "wo", "logit", "prefix"):
                pe.sem_inc(SEMS[name], PER[name])
            for name in ("t_m", "m_done"):
                pe.sem_inc(MOE[name], 2)
            pe.wait_ge(pool_step, 2)

            LAST = B - 1

            def free(uses, banks, b, name, i, second=0):
                n = place(uses, name, i, second)
                b = b - uses[n][2]
                was, j, off = uses[n - len(banks)]
                pe.wait_ge(SEMS[was], nth(was, (b if n >= len(banks) else b - 1) + off, j))
                return banks[n % len(banks)]

            def turn(kind, b, i, src, bank=None):
                if bank is None:
                    bank = free(TP_USES, tp, b, "h_z" if kind == "z" else "l_" + kind, i)
                for k in range(KT):
                    last = nc.tensor.transpose(bank[:, k, :], src[:, k * P:(k + 1) * P], ident[:, :])
                last.then_inc(SEMS["t_" + kind], 1)

            def three(bank, s_hi, s_lo, m_hi, m_lo, chunk0=None):
                for k in range(KT):
                    if chunk0 is not None:
                        pe.wait_ge(w_low, chunk0 + k + 1)
                    nc.tensor.matmul(bank[:, :], s_hi(k), m_hi(k), start=(k == 0), stop=False)
                    nc.tensor.matmul(bank[:, :], s_hi(k), m_lo(k), start=False, stop=False)
                    last = nc.tensor.matmul(bank[:, :], s_lo(k), m_hi(k), start=False, stop=(k == KT - 1))
                return last

            def logits_of(b, t, bank):
                pe.wait_ge(SEMS["h_z"], nth("h_z", b, t))
                for k in range(KT):
                    last = nc.tensor.matmul(bank[:, 0:E], x2T[:, t, k, :], wr_sb[:, k, :], start=(k == 0), stop=(k == KT - 1))
                last.then_inc(SEMS["logit"], 1)

            def prefix_of(b, t, bank):
                pe.wait_ge(SEMS["picked"], nth("picked", b, t))
                nc.tensor.matmul(bank[:, 0:E], before[:, :], members[:, t % 2, :], start=True, stop=True, skip_group_check=True)
                nc.tensor.matmul(bank[:, E:2 * E], ones[:, :], members[:, t % 2, :], start=True, stop=True,
                                 skip_group_check=True).then_inc(SEMS["prefix"], 1)

            def turn_c(b, i):
                pe.wait_ge(ctx_loaded[(i // 2) % 2], b * 32 + 16 * (i // 4 + 1))
                turn("c", b, i, ctx_raw[:, (i // 2) % 2, i % 2, :])

            def keys(b, before_):
                for step, kind, i in KEYS:
                    if before_ is None and (step, i) in CHUNKS and kind in ("", "z"):
                        continue
                    if step == "T" and kind == "c":
                        turn_c(b, i)
                    elif step == "T" and kind == "x":
                        pe.wait_ge(SEMS["xn"], nth("xn", b, i))
                        turn("x", b, i, xn[i])
                    elif step == "T":
                        pe.wait_ge(SEMS["x2n"], nth("x2n", before_, i))
                        turn("z", before_, i, xn[i])
                    elif step == "P":
                        if kind == "k":
                            pe.wait_ge(SEMS["l_c"], nth("l_c", b, i))
                        w = WK if kind == "k" else WV
                        three(free(PJ_USES, pj, b, "expk" if kind == "k" else "v_copied", i),
                              lambda k: ctxT_hi[:, i % 2, k, :], lambda k: ctxT_lo[:, i % 2, k, :],
                              lambda k: w_hi(w)[:, k, :], lambda k: w_lo(w)[:, k, :],
                              KT * w if before_ is None and i == 0 else None).then_inc(SEMS[kind], 1)
                    elif step == "L":
                        logits_of(before_, i, free(PJ_USES, pj, before_, "logit_copied", i))
                    elif step == "K":
                        prefix_of(before_, i, free(PJ_USES, pj, before_, "ranked", i))
                    elif step == "KV":
                        if before_ is None and i == 0:
                            pe.wait_ge(consts, 9)
                        pe.wait_ge(SEMS["khat"], nth("khat", b, i))
                        pe.wait_ge(SEMS["v_copied"], nth("v_copied", b, i))
                        if i == 0:
                            pe.wait_ge(SEMS["kvbd"], nth("kvbd", b, -1))
                        for g in range(G):
                            last = nc.tensor.matmul(kvp[g // 2][:, g % 2, :], khat[:, i % 2, g * P:(g + 1) * P], vones[:, i % 2, g, :],
                                                    start=(i == 0 and g % 2 == 0), stop=(i == ST - 1), skip_group_check=True)
                        last.then_inc(SEMS["kv"], 1)

            def turn_m(m, slot, n):
                pe.wait_ge(xs_loaded[slot], 16 * n + 16)
                pe.wait_ge(MOE["l_m"], mth(m - 2))
                for k in range(KT):
                    last = nc.tensor.transpose(tp[slot][:, k, :], xs_raw[:, slot, k * P:(k + 1) * P], ident[:, :])
                last.then_inc(MOE["t_m"], 1)

            def queries(b):
                for step, kind, i in QUERIES:
                    if step == "Q":
                        if i == 0:
                            pe.wait_ge(SEMS["l_x"], nth("l_x", b, TT - 1))
                        three(free(PJ_USES, pj, b, "expq", i), lambda k: w_hi(WQ)[:, k, i * P:(i + 1) * P], lambda k: w_lo(WQ)[:, k, i * P:(i + 1) * P],
                              lambda k: xT_hi[:, k, :], lambda k: xT_lo[:, k, :]).then_inc(SEMS["q"], 1)
                    elif step == "G":
                        three(free(PJ_USES, pj, b, "biased", i), lambda k: xT_hi[:, k, i * P:(i + 1) * P], lambda k: xT_lo[:, k, i * P:(i + 1) * P],
                              lambda k: w_hi(WG)[:, k, :], lambda k: w_lo(WG)[:, k, :]).then_inc(SEMS["g"], 1)
                    elif step == "A":
                        if i == 0:
                            pe.wait_ge(SEMS["kvbd"], nth("kvbd", b, 0))
                            pe.wait_ge(SEMS["qhat"], nth("qhat", b, G - 1))
                        for h in range(2):
                            bank = free(PJ_USES, pj, b, "ag", i, h)
                            for g in range(2 * h, 2 * h + 2):
                                last = nc.tensor.matmul(bank[:, (g % 2) * CW:(g % 2 + 1) * CW], qhat[:, g, i * P:(i + 1) * P], kvbd[:, g, :],
                                                        start=True, stop=True, skip_group_check=True)
                        last.then_inc(SEMS["at"], 1)
                    elif step == "T" and kind == "c":
                        if b is LAST:
                            pe.wait_ge(SEMS["l_a"], nth("l_a", LAST, 2))
                            turn_m(0, 0, 0)
                        else:
                            turn_c(b + 1, 0)
                    elif step == "T":
                        pe.wait_ge(SEMS["ag"], nth("ag", b, i))
                        turn("a", b, i, num[:, i % 2, :])
                    elif step == "O":
                        pe.wait_ge(SEMS["l_a"], nth("l_a", b, i))
                        three(free(PJ_USES, pj, b, "x2", i), lambda k: agT_hi[:, i % 2, k, :], lambda k: agT_lo[:, i % 2, k, :],
                              lambda k: w_hi(WO)[:, k, :], lambda k: w_lo(WO)[:, k, :]).then_inc(SEMS["wo"], 1)

            pe.wait_ge(ctx_first, 16)
            turn("c", 0, 0, ctx_raw[:, 0, 0, :])
            keys(0, None)
            pe.wait_ge(w_low, 5 * KT)
            with pe.Fori(0, B - 1) as b:
                queries(b)
                keys(b + 1, b)
            queries(B - 1)

            def expert(m, slot):
                e = pe.value_load(tile_expert[0:1, bass.ds(m, 1)], min_val=0, max_val=E - 1)
                pe.wait_ge(we_ready, 2 * e + 2)
                pe.wait_ge(MOE["l_m"], mth(m))
                pe.wait_ge(MOE["y_copied"], mth(m - 2))

                def part(block_of, k):
                    return R[:, bass.ds(block_of, 1), k, :].rearrange("p a d -> p (a d)")

                three(pj[slot], lambda k: xsT_hi[:, slot, k, :], lambda k: xsT_lo[:, slot, k, :],
                      lambda k: part(2 * e, k), lambda k: part(2 * e + 1, k)).then_inc(MOE["m_done"], 1)

            pe.wait_ge(planned, 1)
            pe.wait_ge(SEMS["x2"], nth("x2", LAST, 1))
            pe.wait_ge(SEMS["l_a"], nth("l_a", LAST, TT - 1))
            for step, kind, i in START:
                if step == "T" and kind == "m":
                    turn_m(i, i % 2, i // 2)
                elif step == "M":
                    expert(i, i % 2)
                elif step == "T":
                    pe.wait_ge(SEMS["x2n"], nth("x2n", LAST, i))
                    pe.wait_ge(SEMS["h_z"], nth("h_z", LAST, i - 2))
                    turn("z", LAST, i, xn[i], late_z[i % 2])
                elif step == "L":
                    pe.wait_ge(SEMS["ranked"], nth("ranked", LAST, i - 2)) if i >= 2 else pe.wait_ge(SEMS["x2"], nth("x2", LAST, 2 + i))
                    logits_of(LAST, i, pj[2 + i % 2])
                elif step == "K":
                    pe.wait_ge(SEMS["logit_copied"], nth("logit_copied", LAST, i))
                    prefix_of(LAST, i, pj[2 + i % 2])
            with pe.Fori(0, (FIRST[1] - LOOP1) // 2) as h:
                for s in range(2):
                    turn_m(2 * h + LOOP1 + s + 1, (LOOP1 + s + 1) % 2, h + (LOOP1 + s + 1) // 2)
                    expert(2 * h + LOOP1 + s, (LOOP1 + s) % 2)
            pe.wait_ge(planned, 2)
            for m in range(FIRST[1], LOOP2):
                turn_m(m + 1, (m + 1) % 2, (m + 1) // 2)
                expert(m, m % 2)
            with pe.Fori(0, N_COMB // 2 - 1) as h:
                for s in range(2):
                    turn_m(2 * h + LOOP2 + s + 1, (LOOP2 + s + 1) % 2, h + (LOOP2 + s + 1) // 2)
                    expert(2 * h + LOOP2 + s, (LOOP2 + s) % 2)
            for m in range(M_ALL - 2, M_ALL):
                if m + 1 < M_ALL:
                    turn_m(m + 1, (m + 1) % 2, (m + 1) // 2)
                expert(m, m % 2)


_INS = ["x", "ctx_2048", "L0_xattn_Wq", "L0_xattn_Wg", "L0_xattn_bg", "L0_xattn_Wkv", "L0_xattn_Wo",
        "L0_ffn_Wr", "L0_ffn_We", "L0_ffn_be"]
_TURNED = {"L0_xattn_Wq", "L0_xattn_Wg", "L0_xattn_Wkv", "L0_xattn_Wo"}
_OUTS = [((4, 512, 512), "float32")]


def kernel(**inputs):
    import numpy as _np
    import concourse.bacc as _bacc
    from concourse import mybir as _mybir
    from concourse.bass_utils import run_bass_kernel_spmd as _run

    nc = _bacc.Bacc("TRN2", target_bir_lowering=False, num_devices=1)
    arrays, args = {}, []
    for name in _INS:
        a = _np.ascontiguousarray(_np.asarray(inputs[name]).T if name in _TURNED else inputs[name])
        arrays[f"in_{name}_dram"] = a
        args.append(nc.dram_tensor(f"in_{name}_dram", a.shape, _mybir.dt.from_np(a.dtype), kind="ExternalInput").ap())
    for i, (shape, dtype) in enumerate(_OUTS):
        dt = _mybir.dt.from_np(_np.dtype(dtype))
        args.append(nc.dram_tensor(f"out_{i}_dram", shape, dt, kind="ExternalOutput").ap())
    xattn_moe_kernel(nc, *args)
    r = _run(nc, [arrays], core_ids=[0])
    got = tuple(r.results[0][f"out_{i}_dram"] for i in range(len(_OUTS)))
    return got[0]
```
